# Optimizing a Trainium2 kernel written in Bass

```python
import numpy as np
import jax
import jax.numpy as jnp

def _softmax(x, axis=-1):
    return jax.nn.softmax(x, axis=axis)

def _gelu(x):
    return jax.nn.gelu(x, approximate=True)

def _silu(x):
    return jax.nn.silu(x)

def _sigmoid(x):
    return jax.nn.sigmoid(x)

def _layernorm(x, axis=-1, eps=1e-05):
    m = jnp.mean(x, axis=axis, keepdims=True)
    v = jnp.var(x, axis=axis, keepdims=True)
    return (x - m) / jnp.sqrt(v + eps)

def _scatter_add(tgt, idx, src, axis=0):
    return tgt.at[idx].add(src)

def _segment_sum(src, seg, n):
    return jax.ops.segment_sum(src, seg, n)
kernel_name = 'mk_decoder_preln_d1_seqx_r4_25435a'

def setup_inputs(seed: int=0):
    np.random.seed(seed)
    _w = jnp.asarray

    def _rec_inputs():
        import jax
        import jax.numpy as jnp
        _rk = jax.random.key(seed)
        x = -0.0002928 + 1 * jax.random.normal(jax.random.fold_in(_rk, 1), (8, 512, 256), jnp.float32)
        _lenS = 512 - jax.random.randint(jax.random.fold_in(_rk, 7), (8,), 0, max(1, 512 // 4) + 1, jnp.int32)
        _lenS2 = 64 - jax.random.randint(jax.random.fold_in(_rk, 8), (8,), 0, max(1, 64 // 4) + 1, jnp.int32)
        _ctx_1024P = jax.random.normal(jax.random.fold_in(_rk, 11), (8, 16, 256), jnp.float32)
        _ctx_1024c = jax.random.dirichlet(jax.random.fold_in(_rk, 511), 0.3 * jnp.ones((16,), jnp.float32), (8, 64))
        _ctx_1024t = jnp.einsum('bsk,bkd->bsd', _ctx_1024c, _ctx_1024P)
        _ctx_1024t = _ctx_1024t * jax.lax.rsqrt(jnp.mean(jnp.square(_ctx_1024t)) + 1e-12) * 0.953939
        ctx_1024 = 4.13588e-05 + 0.999923 * (_ctx_1024t + 0.3 * jax.random.normal(jax.random.fold_in(_rk, 611), (8, 64, 256), jnp.float32))
        return (x, ctx_1024)
    x, ctx_1024 = _rec_inputs()

    def _L0_attn_setup():
        import jax, jax.numpy as jnp
        import numpy as np
        NEG = -1000000000.0

        def _attention(x, Wq, bq, Wk, bk, Wv, bv, Wo, num_heads=16):
            B, N, E = x.shape
            H = num_heads
            D = E // H
            scale = D ** (-0.5)
            q = (jnp.einsum('bne,fe->bnf', x, Wq) + bq).reshape(B, N, H, D).transpose(0, 2, 1, 3)
            k = (jnp.einsum('bne,fe->bnf', x, Wk) + bk).reshape(B, N, H, D).transpose(0, 2, 1, 3)
            v = (jnp.einsum('bne,fe->bnf', x, Wv) + bv).reshape(B, N, H, D).transpose(0, 2, 1, 3)
            scores = jnp.einsum('bhqd,bhkd->bhqk', q, k) * scale
            scores = scores.at[:, :, 0, -1].set(NEG)
            scores = scores.at[:, :, -1, 0].set(NEG)
            weights = jax.nn.softmax(scores, axis=-1)
            out = jnp.einsum('bhqk,bhkd->bhqd', weights, v)
            out = out.transpose(0, 2, 1, 3).reshape(B, N, E)
            return jnp.einsum('bne,fe->bnf', out, Wo)
        key = jax.random.key(seed)
        ks = jax.random.split(key, 8)
        B, N, E = (4, 512, 256)
        s = E ** (-0.5)
        return {'x': jax.random.normal(ks[0], (B, N, E), jnp.float32), 'Wq': jax.random.normal(ks[1], (E, E), jnp.float32) * s, 'bq': jax.random.normal(ks[2], (E,), jnp.float32) * 0.02, 'Wk': jax.random.normal(ks[3], (E, E), jnp.float32) * s, 'bk': jax.random.normal(ks[4], (E,), jnp.float32) * 0.02, 'Wv': jax.random.normal(ks[5], (E, E), jnp.float32) * s, 'bv': jax.random.normal(ks[6], (E,), jnp.float32) * 0.02, 'Wo': jax.random.normal(ks[7], (E, E), jnp.float32) * s}
    _L0_attn_all = _L0_attn_setup()
    _L0_attn_in = {k: v for k, v in _L0_attn_all.items() if k in ('Wq', 'bq', 'Wk', 'bk', 'Wv', 'bv', 'Wo')}
    del _L0_attn_all

    def _L0_xattn_setup():
        import jax, jax.numpy as jnp
        import numpy as np
        DIM = 256
        NUM_HEADS = 16
        DIM_HEAD = 64
        INNER = NUM_HEADS * DIM_HEAD
        SCALE = DIM_HEAD ** (-0.5)

        def _layernorm(x, gamma, beta, eps=1e-05):
            mu = jnp.mean(x, axis=-1, keepdims=True)
            var = jnp.mean(jnp.square(x - mu), axis=-1, keepdims=True)
            return (x - mu) * jax.lax.rsqrt(var + eps) * gamma + beta
        key = jax.random.key(seed)
        ks = jax.random.split(key, 8)
        B, SQ, SK = (2, 512, 1024)
        x = jax.random.normal(ks[0], (B, SQ, DIM), dtype=jnp.float32)
        context = jax.random.normal(ks[1], (B, SK, DIM), dtype=jnp.float32)
        ln_gamma = jnp.ones((DIM,), jnp.float32)
        ln_beta = jnp.zeros((DIM,), jnp.float32)
        w_q = jax.random.normal(ks[2], (DIM, INNER), dtype=jnp.float32) / np.sqrt(DIM)
        w_kv = jax.random.normal(ks[3], (DIM, 2 * INNER), dtype=jnp.float32) / np.sqrt(DIM)
        w_out = jax.random.normal(ks[4], (INNER, DIM), dtype=jnp.float32) / np.sqrt(INNER)
        b_out = jnp.zeros((DIM,), jnp.float32)
        gate = jnp.array([0.5], jnp.float32)
        return {'x': x, 'context': context, 'ln_gamma': ln_gamma, 'ln_beta': ln_beta, 'w_q': w_q, 'w_kv': w_kv, 'w_out': w_out, 'b_out': b_out, 'gate': gate}
    _L0_xattn_all = _L0_xattn_setup()
    _L0_xattn_in = {k: v for k, v in _L0_xattn_all.items() if k in ('ln_gamma', 'ln_beta', 'w_q', 'w_kv', 'w_out', 'b_out', 'gate')}
    del _L0_xattn_all

    def _L0_ffn_setup():
        import jax, jax.numpy as jnp
        import numpy as np
        LN_EPS = 1e-05

        def entmax15(z):
            z = z / 2.0
            z = z - jnp.max(z, axis=-1, keepdims=True)
            zs = -jnp.sort(-z, axis=-1)
            k = jnp.arange(1, z.shape[-1] + 1, dtype=z.dtype)
            mean = jnp.cumsum(zs, axis=-1) / k
            meansq = jnp.cumsum(zs * zs, axis=-1) / k
            ss = k * (meansq - jnp.square(mean))
            delta = (1.0 - ss) / k
            tau = mean - jnp.sqrt(jnp.clip(delta, 0.0))
            support = jnp.sum((tau <= zs).astype(jnp.int32), axis=-1, keepdims=True)
            tau_star = jnp.take_along_axis(tau, support - 1, axis=-1)
            return jnp.square(jnp.clip(z - tau_star, 0.0))

        def layernorm_noaffine(v):
            m = jnp.mean(v, axis=-1, keepdims=True)
            var = jnp.mean(jnp.square(v - m), axis=-1, keepdims=True)
            return (v - m) / jnp.sqrt(var + LN_EPS)

        def cp_mumoe(x, gate, Win, Wout):
            ones = jnp.ones(x.shape[:-1] + (1,), x.dtype)
            xb = jnp.concatenate([x, ones], axis=-1)
            z = jnp.einsum('btd,dr->btr', xb, Win) * gate
            return jnp.einsum('btr,or->bto', z, Wout)
        key = jax.random.key(seed)
        ks = jax.random.split(key, 8)
        B, T, D, O, D2, E, R = (8, 512, 256, 1024, 256, 16, 128)
        s = lambda k, shape, scale: jax.random.normal(k, shape, jnp.float32) * scale
        return {'x': s(ks[0], (B, T, D), 1.0), 'proj': s(ks[1], (D, E), D ** (-0.5)), 'C1': s(ks[2], (E, R), E ** (-0.5)), 'Win1': s(ks[3], (D + 1, R), D ** (-0.5)), 'Wout1': s(ks[4], (O, R), R ** (-0.5)), 'C2': s(ks[5], (E, R), E ** (-0.5)), 'Win2': s(ks[6], (O + 1, R), O ** (-0.5)), 'Wout2': s(ks[7], (D2, R), R ** (-0.5))}
    _L0_ffn_all = _L0_ffn_setup()
    _L0_ffn_in = {k: v for k, v in _L0_ffn_all.items() if k in ('proj', 'C1', 'Win1', 'Wout1', 'C2', 'Win2', 'Wout2')}
    del _L0_ffn_all
    return {'x': x, 'ctx_1024': ctx_1024, 'L0_attn_Wq': _L0_attn_in['Wq'], 'L0_attn_bq': _L0_attn_in['bq'], 'L0_attn_Wk': _L0_attn_in['Wk'], 'L0_attn_bk': _L0_attn_in['bk'], 'L0_attn_Wv': _L0_attn_in['Wv'], 'L0_attn_bv': _L0_attn_in['bv'], 'L0_attn_Wo': _L0_attn_in['Wo'], 'L0_xattn_ln_gamma': _L0_xattn_in['ln_gamma'], 'L0_xattn_ln_beta': _L0_xattn_in['ln_beta'], 'L0_xattn_w_q': _L0_xattn_in['w_q'], 'L0_xattn_w_kv': _L0_xattn_in['w_kv'], 'L0_xattn_w_out': _L0_xattn_in['w_out'], 'L0_xattn_b_out': _L0_xattn_in['b_out'], 'L0_xattn_gate': _L0_xattn_in['gate'], 'L0_ffn_proj': _L0_ffn_in['proj'], 'L0_ffn_C1': _L0_ffn_in['C1'], 'L0_ffn_Win1': _L0_ffn_in['Win1'], 'L0_ffn_Wout1': _L0_ffn_in['Wout1'], 'L0_ffn_C2': _L0_ffn_in['C2'], 'L0_ffn_Win2': _L0_ffn_in['Win2'], 'L0_ffn_Wout2': _L0_ffn_in['Wout2']}

def reference(x, ctx_1024, L0_attn_Wq, L0_attn_bq, L0_attn_Wk, L0_attn_bk, L0_attn_Wv, L0_attn_bv, L0_attn_Wo, L0_xattn_ln_gamma, L0_xattn_ln_beta, L0_xattn_w_q, L0_xattn_w_kv, L0_xattn_w_out, L0_xattn_b_out, L0_xattn_gate, L0_ffn_proj, L0_ffn_C1, L0_ffn_Win1, L0_ffn_Wout1, L0_ffn_C2, L0_ffn_Win2, L0_ffn_Wout2):
    import jax
    import jax.numpy as jnp

    def _L0_attn_ref(x, Wq, bq, Wk, bk, Wv, bv, Wo):
        import jax, jax.numpy as jnp
        import numpy as np
        NEG = -1000000000.0

        def _attention(x, Wq, bq, Wk, bk, Wv, bv, Wo, num_heads=16):
            B, N, E = x.shape
            H = num_heads
            D = E // H
            scale = D ** (-0.5)
            q = (jnp.einsum('bne,fe->bnf', x, Wq) + bq).reshape(B, N, H, D).transpose(0, 2, 1, 3)
            k = (jnp.einsum('bne,fe->bnf', x, Wk) + bk).reshape(B, N, H, D).transpose(0, 2, 1, 3)
            v = (jnp.einsum('bne,fe->bnf', x, Wv) + bv).reshape(B, N, H, D).transpose(0, 2, 1, 3)
            scores = jnp.einsum('bhqd,bhkd->bhqk', q, k) * scale
            scores = scores.at[:, :, 0, -1].set(NEG)
            scores = scores.at[:, :, -1, 0].set(NEG)
            weights = jax.nn.softmax(scores, axis=-1)
            out = jnp.einsum('bhqk,bhkd->bhqd', weights, v)
            out = out.transpose(0, 2, 1, 3).reshape(B, N, E)
            return jnp.einsum('bne,fe->bnf', out, Wo)
        return _attention(x, Wq, bq, Wk, bk, Wv, bv, Wo, num_heads=16)

    def _L0_xattn_ref(x, context, ln_gamma, ln_beta, w_q, w_kv, w_out, b_out, gate):
        import jax, jax.numpy as jnp
        import numpy as np
        DIM = 256
        NUM_HEADS = 16
        DIM_HEAD = 64
        INNER = NUM_HEADS * DIM_HEAD
        SCALE = DIM_HEAD ** (-0.5)

        def _layernorm(x, gamma, beta, eps=1e-05):
            mu = jnp.mean(x, axis=-1, keepdims=True)
            var = jnp.mean(jnp.square(x - mu), axis=-1, keepdims=True)
            return (x - mu) * jax.lax.rsqrt(var + eps) * gamma + beta
        B, SQ, _ = x.shape
        SK = context.shape[1]
        xn = _layernorm(x, ln_gamma, ln_beta)
        q = (xn @ w_q).reshape(B, SQ, NUM_HEADS, DIM_HEAD)
        kv = context @ w_kv
        k, v = jnp.split(kv, 2, axis=-1)
        k = k.reshape(B, SK, NUM_HEADS, DIM_HEAD)
        v = v.reshape(B, SK, NUM_HEADS, DIM_HEAD)
        scores = jnp.einsum('bqhd,bkhd->bhqk', q * SCALE, k)
        attn = jax.nn.softmax(scores, axis=-1)
        out = jnp.einsum('bhqk,bkhd->bqhd', attn, v).reshape(B, SQ, INNER)
        out = out @ w_out + b_out
        return out * jnp.tanh(gate[0])

    def _L0_ffn_ref(x, proj, C1, Win1, Wout1, C2, Win2, Wout2):
        import jax, jax.numpy as jnp
        import numpy as np
        LN_EPS = 1e-05

        def entmax15(z):
            z = z / 2.0
            z = z - jnp.max(z, axis=-1, keepdims=True)
            zs = -jnp.sort(-z, axis=-1)
            k = jnp.arange(1, z.shape[-1] + 1, dtype=z.dtype)
            mean = jnp.cumsum(zs, axis=-1) / k
            meansq = jnp.cumsum(zs * zs, axis=-1) / k
            ss = k * (meansq - jnp.square(mean))
            delta = (1.0 - ss) / k
            tau = mean - jnp.sqrt(jnp.clip(delta, 0.0))
            support = jnp.sum((tau <= zs).astype(jnp.int32), axis=-1, keepdims=True)
            tau_star = jnp.take_along_axis(tau, support - 1, axis=-1)
            return jnp.square(jnp.clip(z - tau_star, 0.0))

        def layernorm_noaffine(v):
            m = jnp.mean(v, axis=-1, keepdims=True)
            var = jnp.mean(jnp.square(v - m), axis=-1, keepdims=True)
            return (v - m) / jnp.sqrt(var + LN_EPS)

        def cp_mumoe(x, gate, Win, Wout):
            ones = jnp.ones(x.shape[:-1] + (1,), x.dtype)
            xb = jnp.concatenate([x, ones], axis=-1)
            z = jnp.einsum('btd,dr->btr', xb, Win) * gate
            return jnp.einsum('btr,or->bto', z, Wout)
        a = entmax15(layernorm_noaffine(jnp.einsum('btd,de->bte', x, proj)))
        g1 = jnp.einsum('bte,er->btr', a, C1)
        h = cp_mumoe(x, g1, Win1, Wout1)
        h = jax.nn.gelu(h, approximate=False)
        g2 = jnp.einsum('bte,er->btr', a, C2)
        return cp_mumoe(h, g2, Win2, Wout2)
    x = x + _L0_attn_ref(_layernorm(x, axis=-1), L0_attn_Wq, L0_attn_bq, L0_attn_Wk, L0_attn_bk, L0_attn_Wv, L0_attn_bv, L0_attn_Wo)
    x = x + _L0_xattn_ref(_layernorm(x, axis=-1), ctx_1024, L0_xattn_ln_gamma, L0_xattn_ln_beta, L0_xattn_w_q, L0_xattn_w_kv, L0_xattn_w_out, L0_xattn_b_out, L0_xattn_gate)
    x = x + _L0_ffn_ref(_layernorm(x, axis=-1), L0_ffn_proj, L0_ffn_C1, L0_ffn_Win1, L0_ffn_Wout1, L0_ffn_C2, L0_ffn_Win2, L0_ffn_Wout2)
    return x

_drawn_inputs = setup_inputs


def setup_inputs(seed=0):
    import zlib

    import numpy as np

    out = dict(_drawn_inputs(seed))
    spreads = {'L0_xattn_ln_gamma': (1.0, 0.6),
     'L0_xattn_ln_beta': (0.0, 0.755),
     'L0_xattn_b_out': (0.0, 0.1)}
    factors = {'L0_attn_bq': 8.0,
     'L0_attn_bk': 8.0,
     'L0_attn_bv': 2.915,
     'L0_ffn_proj': 3.857,
     'L0_ffn_C1': 3.915,
     'L0_ffn_Win1': 3.912,
     'L0_ffn_Wout1': 3.929,
     'L0_ffn_C2': 3.597,
     'L0_ffn_Win2': 3.69,
     'L0_ffn_Wout2': 3.718}
    for name, (base, spread) in spreads.items():
        noise = np.random.default_rng([zlib.crc32(name.encode()), seed]).standard_normal(out[name].shape)
        drawn = base * np.exp(spread * noise) if base else spread * noise
        out[name] = jnp.asarray(drawn.astype(out[name].dtype))
    for name, factor in factors.items():
        out[name] = (out[name] * factor).astype(out[name].dtype)
    return out
```

```python
from contextlib import ExitStack

import numpy as np

import concourse.bass as bass
from concourse import mybir
from concourse.alu_op_type import AluOpType as ALU

ACT = mybir.ActivationFunctionType
AX = mybir.AxisListType.X
F32 = mybir.dt.float32
F32R = mybir.dt.float32r

P = 128
B, N, D = 8, 512, 256
H = 16
DH = D // H
SK = 64
XD = 64
INNER = H * XD
R = 128
O = 1024
E = 16
KT = D // P
TT = N // P
CH = 4
HC = H // CH
PAIRS = H // 2
TICKS = CH * TT * HC
VW = 32
EPS = 1e-5
NEG = -4e9
S_PROD = 3 * DH
S_MASK = S_PROD + 2
S_ALL = S_MASK + 2

S_TICK = [[20 + 7 * q + 3 * n for n in range(2)] for q in range(TT)]
T_TICK = [[t + 6 for t in S_TICK[q]] for q in range(TT)]
O_TICK = [T_TICK[q][1] + 2 for q in range(TT)]
X1_TICK = (10, 12)
QK_TICK = (15, 17, 19, 21)
FFN_TICK = 13
_UNITS = ([(t, "V", t) for t in range(2)] + [(1 + q, "OT", q) for q in range(TT)]
          + [(6 + k, "ON", k) for k in range(KT)] + [(9 + n, "WO", n) for n in range(2)]
          + [(8, "AT", 0), (9, "G", 0), (10, "G", 1)] + [(FFN_TICK, "H", m) for m in range(O // P)]
          + [(FFN_TICK + 2, "Y", n) for n in range(2)] + [(17 + k, "X2", k) for k in range(KT)]
          + [(S_TICK[q][n], "S", 2 * q + n) for q in range(TT) for n in range(2)]
          + [(T_TICK[q][n], "T", 2 * q + n) for q in range(TT) for n in range(2)]
          + [(O_TICK[q], "O", q) for q in range(TT)]
          + [(58 + k, "X3", k) for k in range(KT)] + [(61, "Z1", 0)])
PLAN = sorted(_UNITS, key=lambda u: u[0])
FFN_END = ("AT", "G", "H", "Y")
PLAN_FIRST = [u for u in PLAN if u[1] not in FFN_END]
PLAN_LAST = [u for u in PLAN if u[1] != "V"]
PLAN_END = [u for u in PLAN if u[1] in FFN_END]
TICK = {(kind, i): t for t, kind, i in PLAN}
SU_W, SU_O1, SU_O2, SU_BIAS, SU_V, SU_CTX, SU_PAIR = 0, 8, 10, 11, 12, 14, 16
PAIR_UNITS = 11
SETUP_UNITS = SU_PAIR + PAIRS * PAIR_UNITS
MAX_UNITS = HC * TT + 1
EN = 38
EN_VAR, EN_DELTA = 5, EN - 3
CONSTS = 45


class At:

    def __init__(self, reg, off):
        self.reg, self.off = reg, off

    def __add__(self, n):
        return At(self.reg, self.off + n)

    def times(self, k, c):
        return self.off * k + c if self.reg is None else self.reg * k + (self.off * k + c)

    def row(self):
        return bass.ds(self.times(1, 0), 1)


def wait(eng, sem, value):
    if not (isinstance(value, int) and value <= 0):
        eng.wait_ge(sem, value)


def wait_apart(eng, passed, sem, value):
    if not (isinstance(value, int) and value <= 0):
        eng.wait_ge(sem, value)
        eng.sem_inc(passed, 1)


def build_kernel(nc, x, ctx_in, wq, bq, wk, bk, wv, bv, wo, gamma, beta, xwq, xwkv, xwo, xbo, gate,
                 proj, c1, win1, wout1, c2, win2, wout2, out, a_scr, b_scr):
    with ExitStack() as ctx:
        def sb(name, shape, dt=F32):
            return ctx.enter_context(nc.sbuf_tensor(name, shape, dt))

        def sem(name):
            return ctx.enter_context(nc.semaphore(name))

        ident = sb("ident", [P, P])
        w_hi = sb("w_hi", [P, 4, KT, D], F32R)
        w_lo = sb("w_lo", [P, 4, KT, D], F32R)
        bqk = sb("bqk", [P, 4])
        bv_all = sb("bv_all", [P, D])
        bo_all = sb("bo_all", [P, D])
        gate_t = sb("gate_t", [P, 2])
        ln_gb = sb("ln_gb", [P, 2, KT])
        win1_f = sb("win1_f", [P, KT, R])
        win1_hi = sb("win1_hi", [P, KT, R], F32R)
        win1_lo = sb("win1_lo", [P, KT, R], F32R)
        proj_f = sb("proj_f", [P, KT, E])
        proj_hi = sb("proj_hi", [P, KT, E], F32R)
        proj_lo = sb("proj_lo", [P, KT, E], F32R)
        c12 = sb("c12", [E, 2, R])
        wout1_hi = sb("wout1_hi", [P, O], F32R)
        wout1_lo = sb("wout1_lo", [P, O], F32R)
        win2_f = sb("win2_f", [P, O // P, R])
        wout2_t = sb("wout2_t", [P, D])
        zbias = sb("zbias", [P, 2])
        half = sb("half", [P, 2, 4])
        ramp = sb("ramp", [P, TT, E])
        inv_ramp = sb("inv_ramp", [P, TT, E])
        seg = sb("seg", [P, 2, TT, E])

        q_st = sb("q_st", [P, 2 * CH, N], F32R)
        k_st = sb("k_st", [P, 2 * CH, N], F32R)
        qk_hi = sb("qk_hi", [P, 4, N], F32R)
        qk_lo = sb("qk_lo", [P, 4, N], F32R)
        probs = sb("probs", [P, 2, HC, N])
        v_all = sb("v_all", [P, TT, H, VW])
        o_t = sb("o_t", [P, CH, N])
        mx = sb("mx", [P, 2, 16])
        nm = sb("nm", [16, 2, 2, P], F32R)
        xa = sb("xa", [P, TT, D])
        xn1 = sb("xn1", [P, TT, D])
        x1t_hi = sb("x1t_hi", [P, KT, N], F32R)
        x1t_lo = sb("x1t_lo", [P, KT, N], F32R)

        res = sb("res", [P, TT, D])
        res3 = sb("res3", [P, TT, D])
        xn = sb("xn", [P, TT, D])
        xt_hi = sb("xt_hi", [P, KT, N], F32R)
        xt_lo = sb("xt_lo", [P, KT, N], F32R)
        xt_f = sb("xt_f", [P, KT, N])
        a_cat = sb("a_cat", [P, 2, KT, INNER], F32R)
        b_cat = sb("b_cat", [P, PAIRS, D])
        px = sb("px", [P, 2, H, SK])
        pt = sb("pt", [P, 2, PAIRS, P])
        z_hi = sb("z_hi", [P, N], F32R)
        z_lo = sb("z_lo", [P, N], F32R)
        a_sb = sb("a_sb", [P, TT, E])
        stat = sb("stat", [P, 3, TT, 6])
        mv = sb("mv", [P, 3, TT, 2])
        var = sb("var", [P, 3, TT])
        rstd = sb("rstd", [P, 3, TT])
        rc = sb("rc", [P, TT, H])
        cst = sb("cst", [P, 2, 3, 8])
        en = sb("en", [P, 4, TT, E])
        en_s = sb("en_s", [P, 2, TT, E])
        en_c = sb("en_c", [P, 2, TT, E])
        en_m = sb("en_m", [P, 2, TT, E])
        en_v = sb("en_v", [P, 10, TT])
        en_x = sb("en_x", [P, 2, TT, E])

        z1s, z1g, g2s, z2g = (px[:, :, :, :].rearrange("p a h s -> p (a h s)")[:, N * n:N * n + N] for n in range(4))
        pt_rows = pt[:, :, :, :].rearrange("p a b c -> p (a b c)").rearrange("p (n t) -> p n t", t=N)
        h_t = pt_rows[:, 0:2, :]
        a_t = pt_rows[0:E, 2, :]

        w_raw = pt[:, :, :, :].rearrange("p a b c -> p (a b c)").rearrange("p (w k f) -> p w k f", w=4, k=KT)
        wout1_raw = px[:, 0].rearrange("p h s -> p (h s)").rearrange("p (m r) -> p m r", r=R)
        wout2_raw = px[:, 1].rearrange("p h s -> p (h s)")[:, 0:2 * R].rearrange("p (m r) -> p m r", r=R)
        w_st = pt[:, :, :, :].rearrange("p a b c -> p a (b c)").rearrange("p a (w f) -> p a w f", w=4)
        kv_t = px[:, :, :, :].rearrange("p a h s -> p a (h s)").rearrange("p a (w f) -> p a w f", w=2)
        xwq_t = xt_f
        ctx_t = xn[:, :, :].rearrange("p t d -> p (t d)").rearrange("p (k n) -> p k n", k=KT)
        mask_rows = o_t[0:1, :, :]
        ones_row = xn[0:1, 0:2, :].rearrange("p t d -> p (t d)")
        brow = xn[0:1, 2:4, :]
        brow_c = probs[0:1, 0, 0:2, 0:D]
        ctx_raw = res

        st_ps = ctx.enter_context(nc.psum_tensor("st_ps", [P, 2, N], F32))
        sm_ps = ctx.enter_context(nc.psum_tensor("sm_ps", [P, 2, N], F32))
        pv_ps = ctx.enter_context(nc.psum_tensor("pv_ps", [P, N], F32))
        x_ps = ctx.enter_context(nc.psum_tensor("x_ps", [P, N], F32))
        y_ps = ctx.enter_context(nc.psum_tensor("y_ps", [P, 2, N], F32))

        const_ready = sem("const_ready")
        rows_in = sem("rows_in")
        w_in = sem("w_in")
        ws_in = [sem("ws_in0"), sem("ws_in1")]
        small = sem("small")
        tanh_done = sem("tanh_done")
        sp_passed = sem("sp_passed")
        dve_passed = sem("dve_passed")
        bo_done = sem("bo_done")
        w_hi_done = sem("w_hi_done")
        as_out = sem("as_out")
        bs_out = sem("bs_out")
        xa_in = sem("xa_in")
        res_in = sem("res_in")
        a_in = sem("a_in")
        b_in = sem("b_in")
        out_done = sem("out_done")
        refill = [sem(f"refill{c}") for c in range(CH)]
        maxrow = [sem(f"maxrow{c}") for c in range(CH)]
        st_full = sem("st_full")
        exp_done = sem("exp_done")
        pv_done = sem("pv_done")
        ot_done = sem("ot_done")
        sm_full = sem("sm_full")
        sm_taken = sem("sm_taken")
        nm_hi = sem("nm_hi")
        ln_stat = [sem(f"ln_stat{n}") for n in range(3)]
        ln_var = [sem(f"ln_var{n}") for n in range(3)]
        ln_rstd = [sem(f"ln_rstd{n}") for n in range(3)]
        ln_out = [sem(f"ln_out{n}") for n in range(3)]
        t1_full = sem("t1_full")
        t1_hi = sem("t1_hi")
        t1_taken = sem("t1_taken")
        qk_full = sem("qk_full")
        qk_hi_done = sem("qk_hi_done")
        qk_taken = sem("qk_taken")
        pj_full = sem("pj_full")
        pj_taken = sem("pj_taken")
        z2_full = sem("z2_full")
        z2_taken = sem("z2_taken")
        y_full = sem("y_full")
        y_taken = [sem("y_taken0"), sem("y_taken1")]
        rcp = sem("rcp")
        on_hi = sem("on_hi")
        x2_lo = sem("x2_lo")
        x3_hi = sem("x3_hi")
        bo_added = sem("bo_added")
        c_max = sem("c_max")
        c_exp = sem("c_exp")
        c_sum = sem("c_sum")
        c_rcp = sem("c_rcp")
        c_norm = sem("c_norm")
        en_step = sem("en_step")
        en_rstd = sem("en_rstd")
        en_sqrt = sem("en_sqrt")
        zh = sem("zh")
        zl = sem("zl")

        def plan(g):
            if g.reg is not None or 1 <= g.off < B - 1:
                return PLAN
            return {0: PLAN_FIRST, B - 1: PLAN_LAST, B: PLAN_END}[g.off]

        def order(g, kind, i):
            n = [u[1:] for u in plan(g)].index((kind, i))
            if g.reg is None:
                return sum(len(plan(At(None, k))) for k in range(g.off)) + SETUP_UNITS + n
            return SETUP_UNITS + len(PLAN_FIRST) + len(PLAN) * (g.off - 1) + n

        def bank(g, kind, i):
            return order(g, kind, i) % 2

        def y_of(g, kind, i):
            return y_ps[:, bank(g, kind, i)]

        def done(g, kind, i):
            return y_taken[bank(g, kind, i)]

        def nth(g, value, per_plan):
            return value if g.reg is None else g.reg * per_plan + value

        def fill(pe, g, kind, i, after=()):
            n = order(g, kind, i)
            for u in after:
                if bank(g, *u) != n % 2:
                    taken(pe, g, *u)
            wait(pe, y_taken[n % 2], nth(g, n // 2, len(PLAN) // 2))
            return y_ps[:, n % 2]

        def filled(eng, g, kind, i):
            n = order(g, kind, i)
            eng.wait_ge(y_full, nth(g, n + 1, len(PLAN)))
            return y_ps[:, n % 2]

        def taken(eng, g, kind, i):
            n = order(g, kind, i)
            eng.wait_ge(y_taken[n % 2], nth(g, n // 2 + 1, len(PLAN) // 2))

        def has_body(g):
            return ("Z1", 0) in [u[1:] for u in plan(g)]

        def has_end(g):
            return ("AT", 0) in [u[1:] for u in plan(g)]

        def s_fill(pe, u):
            wait(pe, y_taken[u % 2], u // 2)
            return y_ps[:, u % 2]

        def s_filled(eng, u):
            eng.wait_ge(y_full, u + 1)
            return y_ps[:, u % 2]

        def s_taken(eng, u):
            eng.wait_ge(y_taken[u % 2], u // 2 + 1)

        def in_chunk_order(ap):
            return ap.rearrange("p (mc d j) -> p mc j d", j=2, d=DH)

        def in_order(ap):
            return ap.rearrange("p (mc j d) -> p mc j d", j=2, d=DH)

        def head(c, r):
            return 8 * (r % 2) + 2 * c + r // 2

        def ln_bc(ap, n):
            return ap.unsqueeze(2).broadcast_to([P, ap.shape[1], n])

        block = ctx.enter_context(nc.Block())

        @block.sync
        def _(sp):
            def load_xa(a):
                wait_apart(sp, sp_passed, ln_out[0], a.times(4, 0))
                sp.dma_start(xa[:], x[a.row()].rearrange("a (t p) d -> p (a t) d", p=P)).then_inc(xa_in, 16)

            def load_res(g):
                if g.reg is None and g.off == 0:
                    sp.wait_ge(y_full, SU_CTX + KT)
                else:
                    taken(sp, g + -1, "O", 2)
                    sp.sem_inc(sp_passed, 1)
                    taken(sp, g + -1, "O", 3)
                    sp.sem_inc(sp_passed, 1)
                sp.dma_start(res[:], x[g.row()].rearrange("a (t p) d -> p (a t) d", p=P)).then_inc(res_in, 16)

            def load_a(g, first=False):
                if first:
                    sp.wait_ge(as_out, 16 * 4 * PAIRS)
                else:
                    filled(sp, g + -1, "S", 7)
                    sp.sem_inc(sp_passed, 1)
                sp.dma_start(a_cat[:].bitcast(F32), a_scr[g.row()].rearrange("a p h k c -> (a p) h k c")).then_inc(a_in, 16)

            def load_b(g, first=False):
                if first:
                    sp.wait_ge(bs_out, 16 * PAIRS)
                else:
                    filled(sp, g + -1, "O", 3)
                    sp.sem_inc(sp_passed, 1)
                sp.dma_start(b_cat[:], b_scr[g.row()].rearrange("a p h c -> (a p) h c")).then_inc(b_in, 16)

            def fill_stack(a, c):
                wait_apart(sp, sp_passed, qk_taken, a.times(4, 4))
                wait(sp, st_full, (a + -1).times(TICKS, 16 * c + 16))
                for j, st, parts in ((0, q_st, (qk_hi, qk_hi, qk_lo)), (2, k_st, (qk_hi, qk_lo, qk_hi))):
                    for m in range(2):
                        for n, part in enumerate(parts):
                            p0 = 64 * m + DH * n
                            sp.dma_start(st[p0:p0 + DH, 2 * c:2 * c + 2, :].bitcast(F32),
                                         part[32 * c:32 * c + 32, j + m, :].bitcast(F32)).then_inc(refill[c], 16)

            def fill_maxrow(b, c):
                sp.wait_ge(sm_taken, b.times(CH * MAX_UNITS, MAX_UNITS * (c + 1)))
                for m in range(2):
                    for part in range(2):
                        p0 = 64 * m + S_MASK + part
                        sp.dma_start(q_st[p0:p0 + 1, 2 * c:2 * c + 2, :].bitcast(F32),
                                     nm[8 * m:8 * m + 8, c % 2, part, :].bitcast(F32)).then_inc(maxrow[c], 16)

            def load_pair(p):
                if p >= 2:
                    sp.wait_ge(y_full, SU_PAIR + PAIR_UNITS * (p - 1))
                else:
                    sp.wait_ge(y_full, SU_O1)
                cols = slice(P * p, P * p + P)
                t = w_st[:, p % 2]
                sp.dma_start(t[:, 0].rearrange("p (k c) -> p k c", k=KT),
                             xwq[:, cols].rearrange("(k p) c -> p k c", p=P)).then_inc(ws_in[p % 2], 16)
                sp.dma_start(t[:, 1].rearrange("p (k c) -> p k c", k=KT),
                             xwkv[:, cols].rearrange("(k p) c -> p k c", p=P)).then_inc(ws_in[p % 2], 16)
                sp.dma_start(t[:, 2].rearrange("p (k c) -> p k c", k=KT),
                             xwkv[:, INNER + P * p:INNER + P * p + P].rearrange("(k p) c -> p k c", p=P)
                             ).then_inc(ws_in[p % 2], 16)
                sp.dma_start(t[:, 3], xwo[cols, :]).then_inc(ws_in[p % 2], 16)

            def store_a(p, m):
                s_taken(sp, SU_PAIR + PAIR_UNITS * p + 3 + 2 * m)
                s_taken(sp, SU_PAIR + PAIR_UNITS * p + 4 + 2 * m)
                for part in range(2):
                    sp.dma_start(a_scr[:, :, part, m, P * p:P * p + P].rearrange("b p c -> p b c"),
                                 a_cat[:, part, m, :].bitcast(F32).rearrange("p (b c) -> p b c", b=B)
                                 ).then_inc(as_out, 16)

            def store_b(p):
                s_taken(sp, SU_PAIR + PAIR_UNITS * p + 9)
                s_taken(sp, SU_PAIR + PAIR_UNITS * p + 10)
                sp.dma_start(b_scr[:, :, p, :].rearrange("b p c -> p b c"), b_cat[:]).then_inc(bs_out, 16)

            for n, w in enumerate((wq, wk, wv, wo)):
                sp.dma_start(w_raw[:, n], w.rearrange("(f p) e -> p f e", p=P)).then_inc(w_in, 16)
            load_xa(At(None, 0))
            sp.dma_start(wout1_raw, wout1.rearrange("(m p) r -> p m r", p=P)).then_inc(w_in, 16)
            sp.dma_start(wout2_raw, wout2.rearrange("(m p) r -> p m r", p=P)).then_inc(w_in, 16)
            sp.dma_start(brow[:, 0, :], bq.unsqueeze(0)).then_inc(w_in, 16)
            sp.dma_start(brow[:, 1, :], bk.unsqueeze(0)).then_inc(w_in, 16)
            sp.dma_start(bv_all[:], bv.partition_broadcast(P)).then_inc(w_in, 16)
            sp.dma_start(bo_all[:], xbo.partition_broadcast(P)).then_inc(w_in, 16)
            sp.dma_start(gate_t[:, 0:1], gate.partition_broadcast(P)).then_inc(w_in, 16)
            sp.dma_start(ln_gb[:, 0, :], gamma.rearrange("(k p) -> p k", p=P), allow_slow_non_contiguous=True
                         ).then_inc(w_in, 16)
            sp.dma_start(ln_gb[:, 1, :], beta.rearrange("(k p) -> p k", p=P), allow_slow_non_contiguous=True
                         ).then_inc(w_in, 16)
            sp.dma_start(win1_f[:], win1[0:D, :].rearrange("(k p) r -> p k r", p=P)).then_inc(w_in, 16)
            sp.dma_start(zbias[:, 0:1], win1[D:D + 1, :].rearrange("a r -> r a")).then_inc(w_in, 16)
            sp.dma_start(proj_f[:], proj.rearrange("(k p) r -> p k r", p=P)).then_inc(w_in, 16)
            sp.dma_start(c12[:, 0, :], c1).then_inc(w_in, 16)
            sp.dma_start(c12[:, 1, :], c2).then_inc(w_in, 16)
            sp.dma_start(win2_f[:], win2[0:O, :].rearrange("(m p) r -> p m r", p=P)).then_inc(w_in, 16)
            sp.dma_start(zbias[:, 1:2], win2[O:O + 1, :].rearrange("a r -> r a")).then_inc(w_in, 16)
            sp.dma_start(ctx_raw[:], ctx_in.rearrange("(t a) s d -> (a s) t d", a=2)).then_inc(w_in, 16)
            sp.wait_ge(const_ready, CONSTS)
            for m in range(2):
                for st, row, kind in ((q_st, S_PROD, 0), (q_st, S_PROD + 1, 1), (k_st, S_PROD, 2),
                                      (k_st, S_PROD + 1, 3), (k_st, S_MASK, 4), (k_st, S_MASK + 1, 4)):
                    p0 = 64 * m + row
                    sp.dma_start(st[p0:p0 + 1, :, :].bitcast(F32),
                                 (ones_row.unsqueeze(1) if kind == 4 else mask_rows[:, kind:kind + 1, :])
                                 .broadcast_to([1, 2 * CH, N])).then_inc(rows_in, 16)
            for c in range(CH):
                fill_stack(At(None, 0), c)
            load_pair(0)
            load_pair(1)
            for c in range(2):
                fill_maxrow(At(None, 0), c)

            def store(g):
                for n in range(2):
                    taken(sp, g + 1, "Y", n)
                    sp.sem_inc(sp_passed, 1)
                sp.dma_start(out[g.row()].rearrange("a (t p) d -> p (a t) d", p=P), res3[:]).then_inc(out_done, 16)

            def iteration(b, setup=False, store_=True, load=True, project=True):
                if load:
                    load_xa(b + 2)
                if store_:
                    store(b + -2)
                for c in range(CH):
                    if setup:
                        for p in (2 * c, 2 * c + 1):
                            store_a(p, 0)
                            store_a(p, 1)
                            store_b(p)
                            if p + 2 < PAIRS:
                                load_pair(p + 2)
                    if project:
                        fill_stack(b + 1, c)
                    if c < 2:
                        fill_maxrow(b, c + 2)
                    elif project:
                        fill_maxrow(b + 1, c - 2)
                    if c == 3:
                        load_a(b, first=setup)
                        load_b(b, first=setup)
                        load_res(b)

            load_xa(At(None, 1))
            iteration(At(None, 0), setup=True, store_=False)
            iteration(At(None, 1), store_=False)
            with sp.Fori(2, B - 2) as it:
                iteration(At(it, 0))
            iteration(At(None, B - 2), load=False)
            iteration(At(None, B - 1), load=False, project=False)
            store(At(None, B - 2))
            store(At(None, B - 1))
            sp.wait_ge(out_done, 16 * B)

        @block.tensor
        def _(pe):
            def mm(dst, lhs, rhs, start, stop, **kw):
                return nc.tensor.matmul(dst, lhs, rhs, start=start, stop=stop, **kw)

            def mm3(dst, pairs):
                last = None
                for n, (lh, ll, rh, rl) in enumerate(pairs):
                    end = n == len(pairs) - 1
                    mm(dst, lh, rh, n == 0, False)
                    mm(dst, lh, rl, False, False)
                    last = mm(dst, ll, rh, False, end)
                return last

            def scores(b, c, i, r):
                e = 16 * c + 4 * i + r
                if i == 0 and r == 0:
                    pe.wait_ge(maxrow[c], b.times(64, 64))
                wait(pe, exp_done, b.times(TICKS, e - 1))
                m, h = r % 2, 2 * c + r // 2
                rows_ = slice(64 * m, 64 * m + S_ALL)
                mm(st_ps[:, e % 2], k_st[rows_, h, P * i:P * i + P], q_st[rows_, h, :], True, True).then_inc(st_full, 1)

            def values(b, c, i):
                s = 4 * c + i
                pe.wait_ge(exp_done, b.times(TICKS, 4 * s + 4))
                if i == 0:
                    wait(pe, ot_done, b.times(CH, c))
                    if c == 0 and b.reg is None and b.off == 0:
                        s_taken(pe, SU_V)
                        s_taken(pe, SU_V + 1)
                    elif c == 0:
                        taken(pe, b + -1, "V", 0)
                        taken(pe, b + -1, "V", 1)
                for r in range(HC):
                    last = mm(pv_ps[VW * r:VW * r + VW, :], v_all[:, i, head(c, r), :], probs[:, s % 2, r, :],
                              i == 0, i == TT - 1, tile_position=(0, VW * r))
                last.then_inc(pv_done, 1)

            def for_max(b, c, i, r):
                u = MAX_UNITS * c + 4 * i + r
                if i == 0 and r == 0:
                    pe.wait_ge(refill[c], b.times(192, 192))
                wait(pe, sm_taken, b.times(CH * MAX_UNITS, u - 1))
                m, h = r % 2, 2 * c + r // 2
                rows_ = slice(64 * m, 64 * m + S_MASK)
                mm(sm_ps[:, u % 2], q_st[rows_, h, P * i:P * i + P], k_st[rows_, h, :], True, True).then_inc(sm_full, 1)

            def turn_max(b, c):
                u = MAX_UNITS * c + 16
                pe.wait_ge(sm_taken, b.times(CH * MAX_UNITS, u))
                mm(sm_ps[0:16, u % 2, 0:P], mx[:, c % 2, :], ident[:], True, True).then_inc(sm_full, 1)

            def turn_x1(a, k):
                pe.wait_ge(ln_out[0], a.times(4, 4))
                if a.reg is not None or a.off > 2:
                    wait(pe, pj_taken, a.times(1, -2))
                wait(pe, t1_taken, a.times(2, k))
                for t in range(TT):
                    last = nc.tensor.transpose(x_ps[:, P * t:P * t + P], xn1[:, t, P * k:P * k + P], ident[:])
                last.then_inc(t1_full, 1)

            def qk(a, j):
                if j == 0:
                    wait(pe, t1_taken, a.times(2, 2))
                    if a.reg is not None or a.off > 2:
                        wait(pe, z2_taken, a.times(1, -2))
                wait(pe, qk_taken, a.times(4, j))
                cols = slice(P * (j % 2), P * (j % 2) + P)
                mm3(x_ps[:], [(w_hi[:, j // 2, k, cols], w_lo[:, j // 2, k, cols], x1t_hi[:, k, :], x1t_lo[:, k, :])
                              for k in range(KT)]).then_inc(qk_full, 1)

            def v_tiles(y, n):
                for t in (2 * n, 2 * n + 1):
                    tok = slice(P * t, P * t + P)
                    last = mm3(y[:, D * (t % 2):D * (t % 2) + D],
                               [(x1t_hi[:, k, tok], x1t_lo[:, k, tok], w_hi[:, 2, k, :], w_lo[:, 2, k, :])
                                for k in range(KT)])
                last.then_inc(y_full, 1)

            def turn_o(g, t):
                pe.wait_ge(ot_done, g.times(4, 4))
                y = fill(pe, g, "OT", t)
                for c in range(CH):
                    last = nc.tensor.transpose(y[:, P * c:P * c + P], o_t[:, c, P * t:P * t + P], ident[:])
                last.then_inc(y_full, 1)

            def turn_xn(y, k):
                for t in range(TT):
                    last = nc.tensor.transpose(y[:, P * t:P * t + P], xn[:, t, P * k:P * k + P], ident[:])
                last.then_inc(y_full, 1)

            def out_proj(g, n):
                y = fill(pe, g, "WO", n, after=[("ON", 0), ("ON", 1)] if n == 0 else ())
                for t in (2 * n, 2 * n + 1):
                    tok = slice(P * t, P * t + P)
                    last = mm3(y[:, D * (t % 2):D * (t % 2) + D],
                               [(xt_hi[:, k, tok], xt_lo[:, k, tok], w_hi[:, 3, k, :], w_lo[:, 3, k, :])
                                for k in range(KT)])
                last.then_inc(y_full, 1)

            def x_scores(g, q, n):
                if q == 0 and n == 0:
                    pe.wait_ge(x2_lo, g.times(2, 2))
                    pe.wait_ge(a_in, g.times(16, 16))
                y = fill(pe, g, "S", 2 * q + n)
                tok, cols = slice(P * q, P * q + P), slice(N * n, N * n + N)
                mm3(y, [(xt_hi[:, k, tok], xt_lo[:, k, tok], a_cat[:, 0, k, cols], a_cat[:, 1, k, cols])
                        for k in range(KT)]).then_inc(y_full, 1)

            def x_turn(g, q, n):
                pe.wait_ge(c_norm, g.times(8, 2 * q + n + 1))
                y = fill(pe, g, "T", 2 * q + n)
                for p in range(4):
                    h = 8 * n + 2 * p
                    last = nc.tensor.transpose(y[:, P * p:P * p + P], px[:, q % 2, h:h + 2, :].rearrange("p h s -> p (h s)"),
                                               ident[:])
                last.then_inc(y_full, 1)

            def x_out(g, q):
                if q == 0:
                    pe.wait_ge(b_in, g.times(16, 16))
                y = fill(pe, g, "O", q, after=[("T", 2 * q), ("T", 2 * q + 1)])
                for p in range(PAIRS):
                    last = mm(y[:, 0:D], pt[:, q % 2, p, :], b_cat[:, p, :], p == 0, p == PAIRS - 1)
                last.then_inc(y_full, 1)

            def router(g):
                for k in range(KT):
                    taken(pe, g, "X3", k)
                if g.reg is not None or g.off + 2 < B:
                    pe.wait_ge(qk_taken, (g + 2).times(4, 4))
                wait(pe, z2_taken, g.times(1, 0))
                for t in range(TT):
                    tok = slice(P * t, P * t + P)
                    last = mm3(x_ps[:, E * t:E * t + E],
                               [(xt_hi[:, k, tok], xt_lo[:, k, tok], proj_hi[:, k, :], proj_lo[:, k, :])
                                for k in range(KT)])
                last.then_inc(pj_full, 1)

            def z1(g):
                y = fill(pe, g, "Z1", 0)
                mm3(y, [(win1_hi[:, k, :], win1_lo[:, k, :], xt_hi[:, k, :], xt_lo[:, k, :])
                        for k in range(KT)]).then_inc(y_full, 1)

            def turn_a(g):
                pe.wait_ge(en_step, g.times(EN, 0))
                y = fill(pe, g, "AT", 0)
                for t in range(TT):
                    last = mm(y[0:E, P * t:P * t + P], a_sb[:, t, :], ident[:], True, True)
                last.then_inc(y_full, 1)

            def gate_of(g, n):
                y = fill(pe, g, "G", n, after=[("AT", 0)])
                mm(y, c12[:, n, :], a_t, True, True).then_inc(y_full, 1)

            def up(g, m):
                if m == 0:
                    pe.wait_ge(zl, g.times(1, 0))
                    pe.wait_ge(pj_taken, g.times(1, 0))
                    if g.reg is not None or g.off + 2 < B:
                        pe.wait_ge(t1_taken, (g + 2).times(2, 2))
                y = fill(pe, g, "H", m)
                cols = slice(P * m, P * m + P)
                mm3(y, [(wout1_hi[:, cols], wout1_lo[:, cols], z_hi[:], z_lo[:])]).then_inc(y_full, 1)
                for k in ([m - 1] if m > 0 else []) + ([m] if m == O // P - 1 else []):
                    taken(pe, g, "H", k)
                    mm(x_ps[:], win2_f[:, k, :], h_t[:, k % 2, :], k == 0, k == O // P - 1).then_inc(z2_full, 1)

            def result(g, n):
                pe.wait_ge(z2_taken, g.times(1, 0))
                y = fill(pe, g, "Y", n)
                for t in (2 * n, 2 * n + 1):
                    last = mm(y[:, D * (t % 2):D * (t % 2) + D], z2g[:, P * t:P * t + P], wout2_t[:], True, True)
                last.then_inc(y_full, 1)

            def dense(g, t):
                for tick, kind, i in plan(g):
                    if tick != t:
                        continue
                    if kind == "V":
                        v_tiles(fill(pe, g, "V", i), i)
                    if kind == "OT":
                        turn_o(g, i)
                    if kind == "ON":
                        turn_xn(fill(pe, g, "ON", i, after=[("OT", 2), ("OT", 3)] if i == 0 else ()), i)
                    if kind == "WO":
                        out_proj(g, i)
                    if kind == "X2":
                        pe.wait_ge(ln_out[1], g.times(4, 4))
                        turn_xn(fill(pe, g, "X2", i), i)
                    if kind == "S":
                        x_scores(g, i // 2, i % 2)
                    if kind == "T":
                        x_turn(g, i // 2, i % 2)
                    if kind == "O":
                        x_out(g, i)
                    if kind == "X3":
                        pe.wait_ge(ln_out[2], g.times(4, 4))
                        turn_xn(fill(pe, g, "X3", i), i)
                    if kind == "Z1":
                        router(g)
                        z1(g)
                    if kind == "AT":
                        turn_a(g)
                    if kind == "G":
                        gate_of(g, i)
                    if kind == "H":
                        up(g, i)
                    if kind == "Y":
                        result(g, i)

            def projections(b, t):
                if t in X1_TICK:
                    turn_x1(b + 1, X1_TICK.index(t))
                if t in QK_TICK:
                    qk(b + 1, QK_TICK.index(t))

            def turn_pair(y, blocks):
                for f, block_ in enumerate(blocks):
                    last = nc.tensor.transpose(y[:, P * f:P * f + P], block_, ident[:])
                return last

            def setup_weights():
                pe.wait_ge(const_ready, CONSTS)
                pe.wait_ge(w_in, 16 * 21)
                for w in range(4):
                    for k in range(KT):
                        y = s_fill(pe, SU_W + 2 * w + k)
                        turn_pair(y, [w_raw[:, w, f, P * k:P * k + P] for f in range(2)]).then_inc(y_full, 1)
                for n in range(2):
                    y = s_fill(pe, SU_O1 + n)
                    for m in range(4):
                        last = nc.tensor.transpose(y[:, P * m:P * m + P], wout1_raw[:, 4 * n + m, :], ident[:])
                    last.then_inc(y_full, 1)
                y = s_fill(pe, SU_O2)
                for m in range(2):
                    last = nc.tensor.transpose(y[:, P * m:P * m + P], wout2_raw[:, m, :], ident[:])
                last.then_inc(y_full, 1)
                pe.wait_ge(small, 6)
                y = s_fill(pe, SU_BIAS)
                for j in range(4):
                    last = mm(y[:, j:j + 1], brow_c[:, j // 2, P * (j % 2):P * (j % 2) + P], ones_row[:, 0:1], True, True)
                last.then_inc(y_full, 1)

            def setup_ctx(k):
                y = s_fill(pe, SU_CTX + k)
                for t in range(TT):
                    last = nc.tensor.transpose(y[:, P * t:P * t + P], ctx_raw[:, t, P * k:P * k + P], ident[:])
                last.then_inc(y_full, 1)

            def setup_unit(p, n):
                u0 = SU_PAIR + PAIR_UNITS * p
                t = w_st[:, p % 2]
                y = s_fill(pe, u0 + n)
                if n == 0:
                    pe.wait_ge(ws_in[p % 2], 64 * (p // 2 + 1))
                    turn_pair(y, [t[:, 0, P * f:P * f + P] for f in range(2)]).then_inc(y_full, 1)
                if n in (1, 2):
                    for k in range(KT):
                        last = mm(y, t[:, n, P * k:P * k + P], ctx_t[:, k, :], k == 0, k == KT - 1)
                    last.then_inc(y_full, 1)
                if 3 <= n < 7:
                    m, j = (n - 3) // 2, (n - 3) % 2
                    hd = slice(XD * j, XD * j + XD)
                    mm(y, xwq_t[hd, p % 2, P * m:P * m + P], kv_t[hd, p % 2, 0, :], True, True).then_inc(y_full, 1)
                if n >= 7:
                    for b2 in range(2):
                        bb = 2 * (n - 7) + b2
                        for j in range(2):
                            hd = slice(XD * j, XD * j + XD)
                            last = mm(y[hd, D * b2:D * b2 + D], kv_t[hd, p % 2, 1, SK * bb:SK * bb + SK], t[hd, 3, :],
                                      True, True, tile_position=(XD * j, XD * j))
                    last.then_inc(y_full, 1)

            def setup(t):
                if t == 0:
                    setup_ctx(0)
                    setup_ctx(1)
                for n in range(PAIR_UNITS):
                    if t % 8 == (0, 1, 1, 2, 2, 3, 3, 4, 5, 6, 7)[n]:
                        setup_unit(t // 8, n)

            def iteration(b, project=True, has_setup=False):
                for c in range(CH):
                    for i in range(TT):
                        for r in range(HC):
                            t = 16 * c + 4 * i + r
                            scores(b, c, i, r)
                            if r == 1 and t > 4:
                                values(b, (t - 4) // 16, (t - 4) // 4 % 4)
                            if c < 2:
                                for_max(b, c + 2, i, r)
                            elif project:
                                for_max(b + 1, c - 2, i, r)
                            if project:
                                projections(b, t)
                            if has_setup:
                                setup(t)
                            else:
                                dense(b + -1, t)
                    if c < 2:
                        turn_max(b, c + 2)
                    elif project:
                        turn_max(b + 1, c - 2)
                values(b, CH - 1, TT - 1)

            setup_weights()
            first = At(None, 0)
            for k in range(KT):
                turn_x1(first, k)
            for j in range(4):
                qk(first, j)
            for n in range(2):
                v_tiles(s_fill(pe, SU_V + n), n)
            pe.wait_ge(rows_in, 16 * 12)
            for c in range(2):
                for i in range(TT):
                    for r in range(HC):
                        for_max(first, c, i, r)
                turn_max(first, c)
            iteration(first, has_setup=True)
            iteration(At(None, 1))
            with pe.Fori(2, B - 1) as it:
                iteration(At(it, 0))
            iteration(At(None, B - 1), project=False)
            for g in (B - 1, B):
                for t in range(TICKS):
                    dense(At(None, g), t)

        @block.scalar
        def _(act):
            def run(dst, src, f=ACT.Copy, **kw):
                return nc.scalar.activation(dst, src, f, **kw)

            def softmax_exp(b, t):
                act.wait_ge(st_full, b.times(TICKS, t + 1))
                if t % HC == 0:
                    wait(act, pv_done, b.times(16, t // HC - 1))
                run(probs[:, t // HC % 2, t % HC, :], st_ps[:, t % 2], ACT.Exp, scale=DH ** -0.5).then_inc(exp_done, 1)

            def save_chunk(b, c):
                act.wait_ge(pv_done, b.times(16, 4 * c + 4))
                if c == 0 and (b.reg is not None or b.off > 0):
                    filled(act, b + -1, "OT", TT - 1)
                run(o_t[:, c, :], pv_ps[:]).then_inc(ot_done, 1)

            def x1_hi(a, k):
                act.wait_ge(t1_full, a.times(2, k + 1))
                run(x1t_hi[:, k, :], x_ps[:]).then_inc(t1_hi, 1)

            def qk_hi_part(a, j):
                act.wait_ge(qk_full, a.times(4, j + 1))
                if j == 0:
                    for c in range(CH):
                        wait(act, refill[c], a.times(192, 0))
                run(qk_hi[:, j, :], x_ps[:], ACT.Identity, bias=bqk[:, j:j + 1]).then_inc(qk_hi_done, 1)

            def projections(b, t):
                if t in X1_TICK:
                    x1_hi(b + 1, X1_TICK.index(t))
                if t in QK_TICK:
                    qk_hi_part(b + 1, QK_TICK.index(t))

            def dense(g, t):
                for tick, kind, i in plan(g):
                    if tick != t or kind in ("V", "OT", "WO", "S", "O", "Y"):
                        continue
                    if kind == "G" and i == 0:
                        continue
                    y, read = filled(act, g, kind, i), done(g, kind, i)
                    if kind == "ON":
                        run(xt_hi[:, i, :], y).then_inc(on_hi, 1)
                    if kind == "X2":
                        gb = dict(scale=ln_gb[:, 0, i:i + 1], bias=ln_gb[:, 1, i:i + 1])
                        run(xt_hi[:, i, :], y, ACT.Identity, **gb)
                        run(xt_f[:, i, :], y, ACT.Identity, **gb).then_inc(read, 1)
                    if kind == "T":
                        q, n = i // 2, i % 2
                        run(pt[:, q % 2, 4 * n:4 * n + 4, :], y.rearrange("p (a b) -> p a b", b=P)).then_inc(read, 1)
                    if kind == "X3":
                        run(xt_hi[:, i, :], y).then_inc(x3_hi, 1)
                    if kind == "Z1":
                        run(z1s, y, ACT.Identity, bias=zbias[:, 0:1]).then_inc(read, 1)
                    if kind == "AT":
                        run(a_t, y[0:E, :]).then_inc(read, 1)
                    if kind == "G":
                        run(g2s, y).then_inc(read, 1)
                    if kind == "H":
                        wait(act, z2_full, (g + -1).times(O // P, max(i - 1, 0)))
                        run(h_t[:, i % 2, :], y, ACT.Gelu).then_inc(read, 1)
                for q in range(TT):
                    for n in range(2):
                        if t == S_TICK[q][n] + 2 and ("S", 2 * q + n) in [u[1:] for u in plan(g)]:
                            taken(act, g, "S", 2 * q + n)
                            half_px = px[:, q % 2, 8 * n:8 * n + 8, :]
                            run(half_px, half_px, ACT.Exp, scale=XD ** -0.5).then_inc(c_exp, 1)
                if t == TICK["G", 1] + 1 and has_end(g):
                    taken(act, g, "G", 0)
                    run(z_hi[:], z1g).then_inc(zh, 1)

            def setup_unit(p, n):
                u = SU_PAIR + PAIR_UNITS * p + n
                y = s_filled(act, u)
                done = y_taken[u % 2]
                if n == 0:
                    run(xwq_t[:, p % 2, 0:D], y[:, 0:D]).then_inc(done, 1)
                if n in (1, 2):
                    run(kv_t[:, p % 2, n - 1, :], y).then_inc(done, 1)
                if 3 <= n < 7:
                    m, j = (n - 3) // 2, (n - 3) % 2
                    if n == 3:
                        wait(act, as_out, 64 * p)
                    run(a_cat[:, 0, m, :].rearrange("p (b j s) -> p b j s", b=B, j=2)[:, :, j, :],
                        y.rearrange("p (b s) -> p b s", b=B)).then_inc(w_hi_done, 1)
                if n >= 7:
                    if n == 7:
                        wait(act, bs_out, 16 * p)
                    run(b_cat[:, 2 * (n - 7):2 * (n - 7) + 2, :], y.rearrange("p (b f) -> p b f", b=2), ACT.Identity,
                        scale=gate_t[:, 1:2]).then_inc(done, 1)

            def setup(t):
                if t == 0:
                    for k in range(KT):
                        run(ctx_t[:, k, :], s_filled(act, SU_CTX + k)).then_inc(y_taken[k % 2], 1)
                for n in range(PAIR_UNITS):
                    if t % 8 == (0, 1, 1, 2, 2, 3, 3, 4, 5, 6, 7)[n]:
                        setup_unit(t // 8, n)

            def iteration(b, project=True, has_setup=False):
                for t in range(TICKS):
                    softmax_exp(b, t)
                    if t in (18, 34, 50):
                        save_chunk(b, t // 16 - 1)
                    if project:
                        projections(b, t)
                    if has_setup:
                        setup(t)
                    else:
                        dense(b + -1, t)
                save_chunk(b, CH - 1)

            act.wait_ge(w_in, 16 * 21)
            run(gate_t[:, 1:2], gate_t[:, 0:1], ACT.Tanh).then_inc(tanh_done, 1)
            for w in range(4):
                for k in range(KT):
                    y = s_filled(act, SU_W + 2 * w + k)[:, 0:D]
                    dst = w_hi[:, w, k, :]
                    if w < 2:
                        y, dst = in_order(y), in_chunk_order(dst)
                    run(dst, y).then_inc(w_hi_done, 1)
            for n in range(2):
                run(wout1_hi[:, N * n:N * n + N], s_filled(act, SU_O1 + n)).then_inc(w_hi_done, 1)
            run(wout2_t[:], s_filled(act, SU_O2)[:, 0:D]).then_inc(y_taken[SU_O2 % 2], 1)
            run(bqk[:], s_filled(act, SU_BIAS)[:, 0:4]).then_inc(y_taken[SU_BIAS % 2], 1)
            s_taken(act, SU_BIAS)
            for k in range(KT):
                x1_hi(At(None, 0), k)
            for j in range(4):
                qk_hi_part(At(None, 0), j)
            act.wait_ge(tanh_done, 1)
            iteration(At(None, 0), has_setup=True)
            iteration(At(None, 1))
            with act.Fori(2, B - 1) as it:
                iteration(At(it, 0))
            iteration(At(None, B - 1), project=False)
            for g in (B - 1, B):
                for t in range(TICKS):
                    dense(At(None, g), t)

        @block.vector
        def _(dve):
            def minus(dst, a, b):
                return nc.vector.tensor_tensor(dst, a, b, ALU.subtract)

            def lo_part(dst, full, hi):
                return minus(dst, full, hi.bitcast(F32))

            def reduce_max(b, c, i, r):
                u = MAX_UNITS * c + 4 * i + r
                dve.wait_ge(sm_full, b.times(CH * MAX_UNITS, u + 1))
                col = 8 * (r % 2) + 4 * (r // 2) + i
                nc.vector.tensor_reduce(mx[:, c % 2, col:col + 1], sm_ps[:, u % 2], axis=AX, op=ALU.max
                                        ).then_inc(sm_taken, 1)

            def negate_max(b, c):
                u = MAX_UNITS * c + 16
                dve.wait_ge(sm_full, b.times(CH * MAX_UNITS, u + 1))
                if c >= 2:
                    dve.wait_ge(maxrow[c - 2], b.times(64, 64))
                else:
                    wait(dve, maxrow[c + 2], b.times(64, 0))
                src = sm_ps[0:16, u % 2, 0:P]
                nc.vector.tensor_scalar(nm[:, c % 2, 0, :], src, -1.0, None, ALU.mult).then_inc(nm_hi, 1)
                dve.wait_ge(nm_hi, b.times(CH, c + 1))
                nc.vector.scalar_tensor_tensor(out=nm[:, c % 2, 1, :], in0=src, scalar=-1.0,
                                               in1=nm[:, c % 2, 0, :].bitcast(F32), op0=ALU.mult, op1=ALU.subtract
                                               ).then_inc(sm_taken, 1)

            def ln_stats(n, src, b, tiles):
                for t in tiles:
                    nc.vector.bn_stats(stat[:, n, t, :], src[:, t, :]).then_inc(ln_stat[n], 1)

            def ln_moments(n, b):
                wait_apart(dve, dve_passed, ln_stat[n], b.times(8, 4))
                for t in range(TT):
                    nc.vector.bn_aggr(mv[:, n, t, :], stat[:, n, t, :]).then_inc(ln_stat[n], 1)
                dve.wait_ge(ln_stat[n], b.times(8, 8))
                mul, add = (1.0 + EPS, EPS * EPS) if n == 1 else (1.0, EPS)
                nc.vector.tensor_scalar(var[:, n, :], mv[:, n, :, 1], mul, add, ALU.mult, ALU.add).then_inc(ln_var[n], 1)

            def ln_apply(n, dst, src, b, tiles):
                if 0 in tiles:
                    dve.wait_ge(ln_rstd[n], b.times(1, 1))
                for t in tiles:
                    nc.vector.tensor_scalar(dst[:, t, :], src[:, t, :], mv[:, n, t, 0:1], rstd[:, n, t:t + 1],
                                            ALU.subtract, ALU.mult).then_inc(ln_out[n], 1)

            def ln1_a(a):
                dve.wait_ge(xa_in, a.times(16, 16))
                ln_stats(0, xa, a, range(TT))

            def ln1_b(a):
                wait(dve, t1_full, a.times(2, 0))
                ln_apply(0, xn1, xa, a, range(TT))

            def x1_lo(a, k):
                dve.wait_ge(t1_hi, a.times(2, k + 1))
                lo_part(x1t_lo[:, k, :], x_ps[:], x1t_hi[:, k, :]).then_inc(t1_taken, 1)

            def qk_lo_part(a, j):
                dve.wait_ge(qk_hi_done, a.times(4, j + 1))
                nc.vector.scalar_tensor_tensor(out=qk_lo[:, j, :], in0=x_ps[:], scalar=bqk[:, j:j + 1],
                                               in1=qk_hi[:, j, :].bitcast(F32), op0=ALU.add, op1=ALU.subtract
                                               ).then_inc(qk_taken, 1)

            def save_v(y, read, b, n):
                if n == 0:
                    wait(dve, pv_done, b.times(16, 0))
                nc.vector.tensor_tensor(v_all[:, 2 * n:2 * n + 2, :, 0:DH],
                                        y.rearrange("p (t h d) -> p t h d", t=2, d=DH),
                                        bv_all[:].rearrange("p (h d) -> p h d", d=DH).unsqueeze(1)
                                        .broadcast_to([P, 2, H, DH]), ALU.add).then_inc(read, 1)

            def projections(b, t):
                if t == 6:
                    ln1_a(b + 1)
                if t == 7:
                    ln_moments(0, b + 1)
                if t == 9:
                    ln1_b(b + 1)
                if t - 1 in X1_TICK:
                    x1_lo(b + 1, X1_TICK.index(t - 1))
                if t - 1 in QK_TICK:
                    qk_lo_part(b + 1, QK_TICK.index(t - 1))

            def heads_out(g, q):
                y = filled(dve, g, "OT", q).rearrange("p (h w) -> p h w", w=VW)
                nc.vector.reciprocal(rc[:, q, :], y[:, :, DH]).then_inc(rcp, 1)
                dve.wait_ge(rcp, g.times(4, q + 1))
                nc.vector.tensor_tensor(xn[:, q, :].rearrange("p (m cj d) -> p cj m d", m=2, d=DH),
                                        y[:, :, 0:DH].rearrange("p (cj m) d -> p cj m d", m=2),
                                        rc[:, q, :].rearrange("p (cj m) -> p cj m", m=2).unsqueeze(3)
                                        .broadcast_to([P, 2 * CH, 2, DH]), ALU.mult
                                        ).then_inc(done(g, "OT", q), 1)

            def add(dst, src, y, t0, n, read):
                nc.vector.tensor_tensor(dst[:, t0:t0 + n, :], y[:, 0:n * D].rearrange("p (t f) -> p t f", f=D),
                                        src[:, t0:t0 + n, :], ALU.add).then_inc(read, 1)

            def x_center(g, q, n):
                u = ("S", 2 * q + n)
                y = filled(dve, g, *u).rearrange("p (h s) -> p h s", s=SK)
                nc.vector.tensor_reduce(cst[:, n, 0, :], y, axis=AX, op=ALU.max).then_inc(c_max, 1)
                dve.wait_ge(c_max, g.times(8, 2 * q + n + 1))
                minus(px[:, q % 2, 8 * n:8 * n + 8, :], y, ln_bc(cst[:, n, 0, :], SK)).then_inc(done(g, *u), 1)

            def x_sums(g, q, n):
                k = 2 * q + n
                dve.wait_ge(c_exp, g.times(8, k + 1))
                nc.vector.tensor_reduce(cst[:, n, 1, :], px[:, q % 2, 8 * n:8 * n + 8, :], axis=AX, op=ALU.add
                                        ).then_inc(c_sum, 1)
                dve.wait_ge(c_sum, g.times(8, k + 1))
                wait(dve, c_norm, g.times(8, max(k - 1, 0)))
                nc.vector.reciprocal(cst[:, n, 2, :], cst[:, n, 1, :]).then_inc(c_rcp, 1)

            en_n = [0]

            def step(ins):
                en_n[0] += 1
                ins.then_inc(en_step, 1)

            def entmax(g, part):
                V = nc.vector

                def after():
                    dve.wait_ge(en_step, g.times(EN, en_n[0]))

                def after_apart():
                    wait_apart(dve, dve_passed, en_step, g.times(EN, en_n[0]))

                def flat(ap):
                    return ap.rearrange("p a b -> p (a b)")

                if part == 0:
                    en_n[0] = 0
                    s = x_ps[:, 0:TT * E].rearrange("p (t e) -> p t e", e=E)
                    dve.wait_ge(pj_full, g.times(1, 1))
                    step(V.tensor_reduce(en_v[:, 0, :], s, axis=AX, op=ALU.add))
                    after()
                    step(V.tensor_scalar(en_v[:, 1, :], en_v[:, 0, :], 1.0 / E, None, ALU.mult))
                    after()
                    minus(en[:, 0], s, ln_bc(en_v[:, 1, :], E)).then_inc(pj_taken, 1)
                    dve.wait_ge(pj_taken, g.times(1, 1))
                    step(V.tensor_tensor(en[:, 1], en[:, 0], en[:, 0], ALU.mult))
                    after()
                    step(V.tensor_reduce(en_v[:, 2, :], en[:, 1], axis=AX, op=ALU.add))
                    after()
                    step(V.tensor_scalar(en_v[:, 3, :], en_v[:, 2, :], 4.0 / E, 4.0 * EPS, ALU.mult, ALU.add))
                if part == 1:
                    dve.wait_ge(en_rstd, g.times(1, 1))
                    step(V.tensor_tensor(en[:, 2], en[:, 0], ln_bc(en_v[:, 4, :], E), ALU.mult))
                    after()
                    step(V.tensor_reduce(en_v[:, 5, :], en[:, 2], axis=AX, op=ALU.max))
                    after()
                    step(minus(en[:, 0], en[:, 2], ln_bc(en_v[:, 5, :], E)))
                    after_apart()
                    for q in range(TT):
                        step(V.max(en_s[:, 0, q, 0:8], en[:, 0, q, :]))
                    after_apart()
                    for q in range(TT):
                        step(V.match_replace(en[:, 1, q, :], en_s[:, 0, q, 0:8], en[:, 0, q, :], -1e30))
                    after_apart()
                    for q in range(TT):
                        step(V.max(en_s[:, 0, q, 8:16], en[:, 1, q, :]))
                if part == 2:
                    after()
                    step(V.tensor_tensor(en_s[:, 1], en_s[:, 0], en_s[:, 0], ALU.mult))
                    after()
                    step(V.tensor_tensor_scan(en_c[:].rearrange("p a t e -> p (a t e)"),
                                              seg[:].rearrange("p a t e -> p (a t e)"),
                                              en_s[:].rearrange("p a t e -> p (a t e)"), 0.0, ALU.mult, ALU.add))
                    after()
                    step(V.tensor_tensor(en_m[:].rearrange("p a t e -> p a (t e)"),
                                         en_c[:].rearrange("p a t e -> p a (t e)"),
                                         flat(inv_ramp[:]).unsqueeze(1).broadcast_to([P, 2, TT * E]), ALU.mult))
                    after()
                    step(V.tensor_tensor(en[:, 1], en_m[:, 0], en_m[:, 0], ALU.mult))
                    step(minus(en[:, 3], en_m[:, 0], en_s[:, 0]))
                    after()
                    step(minus(en[:, 1], en[:, 1], en_m[:, 1]))
                    step(V.tensor_tensor(en[:, 3], en[:, 3], en[:, 3], ALU.mult))
                    after()
                    step(V.tensor_tensor(en[:, 1], en[:, 1], inv_ramp[:], ALU.add))
                    after()
                    step(V.tensor_scalar(en_m[:, 1], en[:, 1], 0.0, None, ALU.max))
                    after()
                    step(V.tensor_tensor(en[:, 3], en[:, 3], en_m[:, 1], ALU.is_le))
                    after()
                    step(V.tensor_reduce(en_v[:, 6, :], en[:, 3], axis=AX, op=ALU.add))
                if part == 3:
                    after()
                    step(V.tensor_tensor(en[:, 3], ramp[:], ln_bc(en_v[:, 6, :], E), ALU.is_equal))
                    after()
                    step(V.tensor_tensor(en_x[:].rearrange("p a t e -> p a (t e)"),
                                         en_m[:].rearrange("p a t e -> p a (t e)"),
                                         flat(en[:, 3]).unsqueeze(1).broadcast_to([P, 2, TT * E]), ALU.mult))
                    after()
                    step(V.tensor_reduce(en_v[:, 7:9, :], en_x[:], axis=AX, op=ALU.add))
                    after()
                    step(V.tensor_scalar(en_v[:, 3, :], en_v[:, 8, :], 1e-30, None, ALU.max))
                if part == 4:
                    dve.wait_ge(en_sqrt, g.times(1, 1))
                    step(minus(en_v[:, 5, :], en_v[:, 7, :], en_v[:, 9, :]))
                    after()
                    step(minus(en[:, 2], en[:, 0], ln_bc(en_v[:, 5, :], E)))
                    after()
                    step(V.scalar_tensor_tensor(out=a_sb[:], in0=en[:, 2], scalar=0.0, in1=en[:, 2],
                                                op0=ALU.max, op1=ALU.mult))
                    assert en_n[0] == EN, en_n[0]

            def dense(g, t):
                kinds = {u[1:] for u in plan(g)}
                for tick, kind, i in plan(g):
                    if tick != t - 1:
                        continue
                    y, read = y_of(g, kind, i), done(g, kind, i)
                    if kind == "V":
                        save_v(filled(dve, g, kind, i), read, g + 1, i)
                    if kind == "OT":
                        heads_out(g, i)
                    if kind == "ON":
                        dve.wait_ge(on_hi, g.times(2, i + 1))
                        lo_part(xt_lo[:, i, :], y, xt_hi[:, i, :]).then_inc(read, 1)
                    if kind == "WO":
                        if i == 0:
                            dve.wait_ge(res_in, g.times(16, 16))
                        add(res, res, filled(dve, g, kind, i), 2 * i, 2, read)
                    if kind == "X2":
                        taken(dve, g, kind, i)
                        lo_part(xt_lo[:, i, :], xt_f[:, i, :], xt_hi[:, i, :]).then_inc(x2_lo, 1)
                    if kind == "S":
                        x_center(g, i // 2, i % 2)
                    if kind == "O":
                        if i == 0:
                            dve.wait_ge(bo_added, g.times(1, 1))
                            wait(dve, out_done, g.times(16, 0))
                        add(res3, res, filled(dve, g, kind, i), i, 1, read)
                    if kind == "X3":
                        dve.wait_ge(x3_hi, g.times(2, i + 1))
                        lo_part(xt_lo[:, i, :], y, xt_hi[:, i, :]).then_inc(read, 1)
                    if kind == "Y":
                        add(res3, res3, filled(dve, g, kind, i), 2 * i, 2, read)
                if has_body(g):
                    for n in range(2):
                        if t == TICK["WO", n] + 2:
                            taken(dve, g, "WO", n)
                            ln_stats(1, res, g, (2 * n, 2 * n + 1))
                    if t == TICK["WO", 1] + 2:
                        ln_moments(1, g)
                    if t == TICK["WO", 1] + 4:
                        ln_apply(1, xn, res, g, (0, 1))
                    if t == TICK["WO", 1] + 5:
                        ln_apply(1, xn, res, g, (2, 3))
                    for q in range(TT):
                        for n in range(2):
                            if t == S_TICK[q][n] + 3:
                                x_sums(g, q, n)
                        if t == O_TICK[q] + 2:
                            taken(dve, g, "O", q)
                            ln_stats(2, res3, g, (q,))
                    if t == O_TICK[3] + 2:
                        ln_moments(2, g)
                    if t == O_TICK[3] + 4:
                        ln_apply(2, xn, res3, g, range(TT))
                    if t == TICK["Z1", 0] + 1:
                        entmax(g, 0)
                if has_end(g):
                    if t in (1, 3, 5, 7):
                        entmax(g + -1, (t + 1) // 2)
                    if t == TICK["G", 0] + 1:
                        y = filled(dve, g, "G", 0)
                        taken(dve, g + -1, "Z1", 0)
                        nc.vector.tensor_tensor(z1g, y, z1s, ALU.mult).then_inc(done(g, "G", 0), 1)
                    if t == TICK["G", 1] + 2:
                        dve.wait_ge(zh, g.times(1, 0))
                        lo_part(z_lo[:], z1g, z_hi[:]).then_inc(zl, 1)
                    if t == FFN_TICK + 1:
                        dve.wait_ge(z2_full, g.times(O // P, 0))
                        taken(dve, g, "G", 1)
                        nc.vector.scalar_tensor_tensor(out=z2g, in0=x_ps[:], scalar=zbias[:, 1:2], in1=g2s,
                                                       op0=ALU.add, op1=ALU.mult).then_inc(z2_taken, 1)

            def setup(t):
                p = t // 8
                for n in range(3, 7):
                    if t % 8 == (2, 2, 3, 3)[n - 3]:
                        m, j = (n - 3) // 2, (n - 3) % 2
                        u = SU_PAIR + PAIR_UNITS * p + n
                        dve.wait_ge(w_hi_done, 10 + 4 * p + n - 2)
                        if n == 3:
                            wait(dve, as_out, 64 * p)
                        dst, hi = (a_cat[:, part, m, :].rearrange("p (b j s) -> p b j s", b=B, j=2)[:, :, j, :]
                                   for part in (1, 0))
                        lo_part(dst, y_ps[:, u % 2].rearrange("p (b s) -> p b s", b=B), hi).then_inc(y_taken[u % 2], 1)

            def iteration(b, project=True, has_setup=False):
                for t in range(TICKS):
                    c, i, r = t // 16, t // 4 % 4, t % 4
                    if c < 2:
                        reduce_max(b, c + 2, i, r)
                    elif project:
                        reduce_max(b + 1, c - 2, i, r)
                    if project:
                        projections(b, t)
                    if has_setup:
                        setup(t)
                    else:
                        dense(b + -1, t)
                    if r == 3 and i == 3:
                        if c < 2:
                            negate_max(b, c + 2)
                        elif project:
                            negate_max(b + 1, c - 2)

            dve.wait_ge(w_in, 16 * 21)
            nc.vector.tensor_copy(win1_hi[:], win1_f[:]).then_inc(small, 1)
            nc.vector.tensor_copy(proj_hi[:], proj_f[:]).then_inc(small, 1)
            dve.wait_ge(small, 2)
            lo_part(win1_lo[:], win1_f[:], win1_hi[:]).then_inc(small, 1)
            lo_part(proj_lo[:], proj_f[:], proj_hi[:]).then_inc(small, 1)
            for n in range(2):
                nc.vector.tensor_copy(in_chunk_order(brow_c[:, n, :]), in_order(brow[:, n, :])).then_inc(small, 1)
            for w in range(4):
                for k in range(KT):
                    u = SU_W + 2 * w + k
                    dve.wait_ge(w_hi_done, u + 1)
                    y, dst, hi = y_ps[:, u % 2, 0:D], w_lo[:, w, k, :], w_hi[:, w, k, :]
                    if w < 2:
                        y, dst, hi = in_order(y), in_chunk_order(dst), in_chunk_order(hi)
                    lo_part(dst, y, hi).then_inc(y_taken[u % 2], 1)
            first = At(None, 0)
            ln1_a(first)
            for n in range(2):
                dve.wait_ge(w_hi_done, SU_O1 + n + 1)
                lo_part(wout1_lo[:, N * n:N * n + N], y_ps[:, n % 2], wout1_hi[:, N * n:N * n + N]
                        ).then_inc(y_taken[n % 2], 1)
            ln_moments(0, first)
            ln1_b(first)
            for k in range(KT):
                x1_lo(first, k)
            s_taken(dve, SU_BIAS)
            for j in range(4):
                qk_lo_part(first, j)
            dve.wait_ge(const_ready, CONSTS)
            for n in range(2):
                save_v(s_filled(dve, SU_V + n), y_taken[n], first, n)
            for c in range(2):
                for i in range(TT):
                    for r in range(HC):
                        reduce_max(first, c, i, r)
                negate_max(first, c)
            iteration(first, has_setup=True)
            iteration(At(None, 1))
            with dve.Fori(2, B - 1) as it:
                iteration(At(it, 0))
            iteration(At(None, B - 1), project=False)
            for g in (B - 1, B):
                for t in range(TICKS):
                    dense(At(None, g), t)

        @block.gpsimd
        def _(gp):
            G = nc.gpsimd

            def const(ins):
                ins.then_inc(const_ready, 1)

            def deviation(n, b):
                gp.wait_ge(ln_var[n], b.times(1, 1))
                G.tensor_tensor(rstd[:, n, :], var[:, n, :], half[:, 0, :], ALU.pow).then_inc(ln_rstd[n], 1)

            def entmax_powers(g):
                gp.wait_ge(en_step, g.times(EN, EN_VAR))
                G.tensor_tensor(en_v[:, 4, :], en_v[:, 3, :], half[:, 0, :], ALU.pow).then_inc(en_rstd, 1)
                gp.wait_ge(en_step, g.times(EN, EN_DELTA))
                G.tensor_tensor(en_v[:, 9, :], en_v[:, 3, :], half[:, 1, :], ALU.pow).then_inc(en_sqrt, 1)

            def dense(g):
                deviation(1, g)
                gp.wait_ge(ln_out[1], g.times(4, 4))
                G.tensor_tensor(res[:], res[:], bo_all[:].unsqueeze(1).broadcast_to([P, TT, D]), ALU.add
                                ).then_inc(bo_added, 1)
                for q in range(TT):
                    for n in range(2):
                        gp.wait_ge(c_rcp, g.times(8, 2 * q + n + 1))
                        part = px[:, q % 2, 8 * n:8 * n + 8, :]
                        G.tensor_tensor(part, part, ln_bc(cst[:, n, 2, :], SK), ALU.mult).then_inc(c_norm, 1)
                deviation(2, g)

            const(G.memset(ident[:], 0.0))
            const(G.memset(half[:, 0, :], -0.5))
            const(G.memset(half[:, 1, :], 0.5))
            const(G.memset(mask_rows, 0.0))
            const(G.memset(seg[:], 1.0))
            const(G.memset(v_all[:, :, :, DH:VW], 1.0))
            for k in range(E):
                const(G.memset(ramp[:, :, k:k + 1], float(k + 1)))
                const(G.memset(inv_ramp[:, :, k:k + 1], 1.0 / (k + 1)))
            gp.wait_ge(const_ready, 6 + 2 * E)
            const(G.affine_select(out=ident[:], in_=ident[:], compare_op=ALU.not_equal, fill=1.0, base=0,
                                  pattern=[[-1, P]], channel_multiplier=1))
            const(G.memset(mask_rows[:, 0, 0:1], 1.0))
            const(G.memset(mask_rows[:, 1, N - 1:N], 1.0))
            const(G.memset(mask_rows[:, 2, N - 1:N], NEG))
            const(G.memset(mask_rows[:, 3, 0:1], NEG))
            const(G.memset(ones_row, 1.0))
            const(G.memset(seg[:, :, :, 0:1], 0.0))
            deviation(0, At(None, 0))
            gp.wait_ge(tanh_done, 1)
            G.tensor_scalar(bo_all[:], bo_all[:], gate_t[:, 1:2], None, ALU.mult).then_inc(bo_done, 1)
            gp.wait_ge(bo_done, 1)
            deviation(0, At(None, 1))
            deviation(0, At(None, 2))
            dense(At(None, 0))
            with gp.Fori(2, B - 1) as it:
                entmax_powers(At(it, -2))
                deviation(0, At(it, 1))
                dense(At(it, -1))
            for g in (B - 2, B - 1):
                entmax_powers(At(None, g - 1))
                dense(At(None, g))
            entmax_powers(At(None, B - 1))


_INS = ["x", "ctx_1024", "L0_attn_Wq", "L0_attn_bq", "L0_attn_Wk", "L0_attn_bk", "L0_attn_Wv", "L0_attn_bv",
        "L0_attn_Wo", "L0_xattn_ln_gamma", "L0_xattn_ln_beta", "L0_xattn_w_q", "L0_xattn_w_kv", "L0_xattn_w_out",
        "L0_xattn_b_out", "L0_xattn_gate", "L0_ffn_proj", "L0_ffn_C1", "L0_ffn_Win1", "L0_ffn_Wout1", "L0_ffn_C2",
        "L0_ffn_Win2", "L0_ffn_Wout2"]


def kernel(**inputs):
    import concourse.bacc as bacc
    from concourse.bass_utils import run_bass_kernel_spmd

    nc = bacc.Bacc("TRN2", target_bir_lowering=False, num_devices=1)
    arrays, args = {}, []
    for name in _INS:
        a = np.ascontiguousarray(inputs[name])
        arrays[f"in_{name}"] = a
        args.append(nc.dram_tensor(f"in_{name}", a.shape, F32, kind="ExternalInput").ap())
    out = nc.dram_tensor("out_x", (B, N, D), F32, kind="ExternalOutput").ap()
    a_scr = nc.dram_tensor("a_scr", (B, P, 2, KT, INNER), F32, kind="Internal").ap()
    b_scr = nc.dram_tensor("b_scr", (B, P, PAIRS, D), F32, kind="Internal").ap()
    build_kernel(nc, *args, out, a_scr, b_scr)
    r = run_bass_kernel_spmd(nc, [arrays], core_ids=[0])
    return r.results[0]["out_x"]
```

```python
from contextlib import ExitStack

import numpy as np

import concourse.bass as bass
from concourse import mybir
from concourse.alu_op_type import AluOpType as ALU

ACT = mybir.ActivationFunctionType
AX = mybir.AxisListType.X
F32 = mybir.dt.float32
F32R = mybir.dt.float32r

P = 128
B, N, D = 8, 512, 256
H = 16
DH = D // H
SK = 64
XD = 64
INNER = H * XD
R = 128
O = 1024
E = 16
KT = D // P
TT = N // P
CH = 4
HC = H // CH
PAIRS = H // 2
TICKS = CH * TT * HC
VW = 32
EPS = 1e-5
NEG = -4e9
S_PROD = 3 * DH
S_MASK = S_PROD + 2
S_ALL = S_MASK + 2

V_TICK = (0, 2)
OT_TICK = (2, 3, 5, 5)
ON_TICK = (7, 8)
WO_TICK = (10, 11)
X2_TICK = (16, 16)
S_TICK = ((20, 23), (27, 30), (34, 37), (41, 44))
T_TICK = ((26, 29), (33, 36), (40, 43), (47, 50))
O_TICK = (31, 38, 45, 52)
X3_TICK = (58, 59)
Z1_TICK = 62
AT_TICK = 10
G_TICK = (12, 13)
FFN_TICK = (15, 15, 15, 15, 19, 19, 19, 19)
Y_TICK = (21, 23)
X1_TICK = (1, 3)
QK_TICK = (7, 9, 11, 13)
LN1_TICK = (48, 50, 52)
LN2_TICK = (13, 15, 15)
LN3_TICK = (54, 56)
EN_TICK = (0, 1, 1, 5, 7, 9)
SUM_TICK = ((23, 26), (30, 33), (37, 40), (44, 47))
ZH_TICK = 12
ZL_TICK = 14
Z2_TICK = 20
_UNITS = ([(t, "V", i) for i, t in enumerate(V_TICK)] + [(t, "OT", i) for i, t in enumerate(OT_TICK)]
          + [(t, "ON", i) for i, t in enumerate(ON_TICK)] + [(AT_TICK, "AT", 0)]
          + [(t, "WO", i) for i, t in enumerate(WO_TICK)] + [(t, "G", i) for i, t in enumerate(G_TICK)]
          + [(t, "H", i) for i, t in enumerate(FFN_TICK)] + [(t, "Y", i) for i, t in enumerate(Y_TICK)]
          + [(t, "X2", i) for i, t in enumerate(X2_TICK)]
          + [(S_TICK[q][n], "S", 2 * q + n) for q in range(TT) for n in range(2)]
          + [(T_TICK[q][n], "T", 2 * q + n) for q in range(TT) for n in range(2)]
          + [(t, "O", i) for i, t in enumerate(O_TICK)]
          + [(t, "X3", i) for i, t in enumerate(X3_TICK)] + [(Z1_TICK, "Z1", 0)])
PLAN = sorted(_UNITS, key=lambda u: u[0])
FFN_END = ("AT", "G", "H", "Y")
PLAN_FIRST = [u for u in PLAN if u[1] not in FFN_END]
PLAN_LAST = [u for u in PLAN if u[1] != "V"]
PLAN_END = [u for u in PLAN if u[1] in FFN_END]
SU_W, SU_BIAS, SU_O1, SU_O2, SU_V, SU_CTX, SU_PAIR = (0, 1, 2, 3, 5, 6, 7, 8), 4, 9, 11, 12, 14, 16
PAIR_UNITS = 11
PAIR_TICKS = (0, 1, 2, 4, 5, 6, 7, 8, 9, 10, 11)
SETUP_TICKS = 2 * TT * HC
SETUP_UNITS = SU_PAIR + PAIRS * PAIR_UNITS
MAX_UNITS = HC * TT + 1
EN = 38
EN_VAR, EN_DELTA = 6, EN - 3
CONSTS = 46


class At:

    def __init__(self, reg, off):
        self.reg, self.off = reg, off

    def __add__(self, n):
        return At(self.reg, self.off + n)

    def times(self, k, c):
        return self.off * k + c if self.reg is None else self.reg * k + (self.off * k + c)

    def row(self):
        return bass.ds(self.times(1, 0), 1)


def wait(eng, sem, value):
    if not (isinstance(value, int) and value <= 0):
        eng.wait_ge(sem, value)


def wait_apart(eng, passed, sem, value):
    if not (isinstance(value, int) and value <= 0):
        eng.wait_ge(sem, value)
        eng.sem_inc(passed, 1)


def build_kernel(nc, x, ctx_in, wq, bq, wk, bk, wv, bv, wo, gamma, beta, xwq, xwkv, xwo, xbo, gate,
                 proj, c1, win1, wout1, c2, win2, wout2, out, a_scr, b_scr):
    with ExitStack() as ctx:
        def sb(name, shape, dt=F32):
            return ctx.enter_context(nc.sbuf_tensor(name, shape, dt))

        def sem(name):
            return ctx.enter_context(nc.semaphore(name))

        ident = sb("ident", [P, P])
        w_hi = sb("w_hi", [P, 4, KT, D], F32R)
        w_lo = sb("w_lo", [P, 4, KT, D], F32R)
        bqkv = sb("bqkv", [P, 6])
        bv_row = sb("bv_row", [1, D])
        bo_all = sb("bo_all", [P, D])
        gate_t = sb("gate_t", [P, 2])
        ln_gb = sb("ln_gb", [P, 2, KT])
        win1_f = sb("win1_f", [P, KT, R])
        win1_hi = sb("win1_hi", [P, KT, R], F32R)
        win1_lo = sb("win1_lo", [P, KT, R], F32R)
        proj_f = sb("proj_f", [P, KT, E])
        proj_hi = sb("proj_hi", [P, KT, E], F32R)
        proj_lo = sb("proj_lo", [P, KT, E], F32R)
        c12 = sb("c12", [E, 2, R])
        wout1_hi = sb("wout1_hi", [P, O], F32R)
        wout1_lo = sb("wout1_lo", [P, O], F32R)
        win2_f = sb("win2_f", [P, O // P, R])
        wout2_t = sb("wout2_t", [P, D])
        zbias = sb("zbias", [P, 2])
        half = sb("half", [P, 2, 4])
        ramp = sb("ramp", [P, TT, E])
        inv_ramp = sb("inv_ramp", [P, TT, E])
        seg = sb("seg", [P, 2, TT, E])

        q_st = sb("q_st", [P, 2 * CH, N], F32R)
        k_st = sb("k_st", [P, 2 * CH, N], F32R)
        qk_hi = sb("qk_hi", [P, 4, N], F32R)
        qk_lo = sb("qk_lo", [P, 4, N], F32R)
        probs = sb("probs", [P, 2, HC, N])
        v_all = sb("v_all", [P, TT, H, VW])
        o_t = sb("o_t", [P, CH, N])
        mx = sb("mx", [P, 2, 16])
        nm = sb("nm", [16, 2, 2, P], F32R)
        xa = sb("xa", [P, TT, D])
        xn1 = sb("xn1", [P, TT, D])
        x1t_hi = sb("x1t_hi", [P, KT, N], F32R)
        x1t_lo = sb("x1t_lo", [P, KT, N], F32R)

        res = sb("res", [P, TT, D])
        res3 = sb("res3", [P, TT, D])
        xn = sb("xn", [P, TT, D])
        xt_hi = sb("xt_hi", [P, KT, N], F32R)
        xt_lo = sb("xt_lo", [P, KT, N], F32R)
        xt_f = sb("xt_f", [P, KT, N])
        a_cat = sb("a_cat", [P, 2, KT, INNER], F32R)
        b_cat = sb("b_cat", [P, PAIRS, D])
        px = sb("px", [P, 2, H, SK])
        pt = sb("pt", [P, 2, PAIRS, P])
        z_hi = sb("z_hi", [P, N], F32R)
        z_lo = sb("z_lo", [P, N], F32R)
        a_sb = sb("a_sb", [P, TT, E])
        table_pad = sb("table_pad", [P, 2])
        stat = sb("stat", [P, 3, TT, 6])
        mv = sb("mv", [P, 3, TT, 2])
        var = sb("var", [P, 3, TT])
        rstd = sb("rstd", [P, 3, TT])
        rc = sb("rc", [P, TT, H])
        cst = sb("cst", [P, 2, 3, 8])
        en = sb("en", [P, 4, TT, E])
        en_s = sb("en_s", [P, 2, TT, E])
        en_c = sb("en_c", [P, 2, TT, E])
        en_m = sb("en_m", [P, 2, TT, E])
        en_v = sb("en_v", [P, 10, TT])
        en_x = sb("en_x", [P, 2, TT, E])

        z1s, z1g, g2s, z2g = (px[:, :, :, :].rearrange("p a h s -> p (a h s)")[:, N * n:N * n + N] for n in range(4))
        pt_rows = pt[:, :, :, :].rearrange("p a b c -> p (a b c)").rearrange("p (n t) -> p n t", t=N)
        h_t = pt_rows[:, 0:2, :]
        a_t = pt_rows[0:E, 2, :]

        w_raw = pt[:, :, :, :].rearrange("p a b c -> p (a b c)").rearrange("p (w k f) -> p w k f", w=4, k=KT)
        wout1_raw = px[:, 0].rearrange("p h s -> p (h s)").rearrange("p (m r) -> p m r", r=R)
        wout2_raw = px[:, 1].rearrange("p h s -> p (h s)")[:, 0:2 * R].rearrange("p (m r) -> p m r", r=R)
        w_st = pt[:, :, :, :].rearrange("p a b c -> p a (b c)").rearrange("p a (w f) -> p a w f", w=4)
        kv_t = px[:, :, :, :].rearrange("p a h s -> p a (h s)").rearrange("p a (w f) -> p a w f", w=2)
        xwq_t = xt_f
        ctx_t = xn[:, :, :].rearrange("p t d -> p (t d)").rearrange("p (k n) -> p k n", k=KT)
        mask_rows = o_t[0:1, :, :]
        ones_row = xn[0:1, 0:2, :].rearrange("p t d -> p (t d)")
        brow = xn[0:1, 2:4, :]
        brow_c = probs[0:1, 0, 0:2, 0:D]
        ctx_raw = res

        st_ps = ctx.enter_context(nc.psum_tensor("st_ps", [P, 2, N], F32))
        sm_ps = ctx.enter_context(nc.psum_tensor("sm_ps", [P, 2, N], F32))
        pv_ps = ctx.enter_context(nc.psum_tensor("pv_ps", [P, N], F32))
        x_ps = ctx.enter_context(nc.psum_tensor("x_ps", [P, N], F32))
        y_ps = ctx.enter_context(nc.psum_tensor("y_ps", [P, 2, N], F32))

        const_ready = sem("const_ready")
        rows_in = sem("rows_in")
        qk_in = sem("qk_in")
        w_in = sem("w_in")
        ws_in = [sem("ws_in0"), sem("ws_in1")]
        small = sem("small")
        tanh_done = sem("tanh_done")
        sp_passed = sem("sp_passed")
        dve_passed = sem("dve_passed")
        bo_done = sem("bo_done")
        w_hi_done = sem("w_hi_done")
        as_out = sem("as_out")
        bs_out = sem("bs_out")
        xa_in = sem("xa_in")
        res_in = sem("res_in")
        a_in = sem("a_in")
        b_in = sem("b_in")
        out_done = sem("out_done")
        refill = [sem(f"refill{c}") for c in range(CH)]
        maxrow = [sem(f"maxrow{c}") for c in range(CH)]
        st_full = sem("st_full")
        exp_done = sem("exp_done")
        pv_done = sem("pv_done")
        ot_done = sem("ot_done")
        sm_full = sem("sm_full")
        sm_taken = sem("sm_taken")
        nm_hi = sem("nm_hi")
        ln_stat = [sem(f"ln_stat{n}") for n in range(3)]
        ln_var = [sem(f"ln_var{n}") for n in range(3)]
        ln_rstd = [sem(f"ln_rstd{n}") for n in range(3)]
        ln_out = [sem(f"ln_out{n}") for n in range(3)]
        t1_full = sem("t1_full")
        t1_hi = sem("t1_hi")
        t1_taken = sem("t1_taken")
        qk_full = sem("qk_full")
        qk_hi_done = sem("qk_hi_done")
        qk_taken = sem("qk_taken")
        pj_full = sem("pj_full")
        pj_taken = sem("pj_taken")
        z2_full = sem("z2_full")
        z2_taken = sem("z2_taken")
        y_full = sem("y_full")
        y_taken = [sem("y_taken0"), sem("y_taken1")]
        rcp = sem("rcp")
        on_hi = sem("on_hi")
        x2_lo = sem("x2_lo")
        x3_hi = sem("x3_hi")
        bo_added = sem("bo_added")
        c_max = sem("c_max")
        c_exp = sem("c_exp")
        c_sum = sem("c_sum")
        c_rcp = sem("c_rcp")
        c_norm = sem("c_norm")
        en_step = sem("en_step")
        en_rstd = sem("en_rstd")
        en_sqrt = sem("en_sqrt")
        zh = sem("zh")
        zl = sem("zl")

        def plan(g):
            if g.reg is not None or 1 <= g.off < B - 1:
                return PLAN
            return {0: PLAN_FIRST, B - 1: PLAN_LAST, B: PLAN_END}[g.off]

        def order(g, kind, i):
            n = [u[1:] for u in plan(g)].index((kind, i))
            if g.reg is None:
                return sum(len(plan(At(None, k))) for k in range(g.off)) + SETUP_UNITS + n
            return SETUP_UNITS + len(PLAN_FIRST) + len(PLAN) * (g.off - 1) + n

        def bank(g, kind, i):
            return order(g, kind, i) % 2

        def y_of(g, kind, i):
            return y_ps[:, bank(g, kind, i)]

        def done(g, kind, i):
            return y_taken[bank(g, kind, i)]

        def nth(g, value, per_plan):
            return value if g.reg is None else g.reg * per_plan + value

        def fill(pe, g, kind, i, after=()):
            n = order(g, kind, i)
            for u in after:
                if bank(g, *u) != n % 2:
                    taken(pe, g, *u)
            wait(pe, y_taken[n % 2], nth(g, n // 2, len(PLAN) // 2))
            return y_ps[:, n % 2]

        def filled(eng, g, kind, i):
            n = order(g, kind, i)
            eng.wait_ge(y_full, nth(g, n + 1, len(PLAN)))
            return y_ps[:, n % 2]

        def taken(eng, g, kind, i):
            n = order(g, kind, i)
            eng.wait_ge(y_taken[n % 2], nth(g, n // 2 + 1, len(PLAN) // 2))

        def is_last(g):
            return g.reg is None and g.off == B - 1

        def x_divide(engine, q, n):
            part = px[:, q % 2, 8 * n:8 * n + 8, :]
            return engine.tensor_tensor(part, part, ln_bc(cst[:, n, 2, :], SK), ALU.mult)

        def is_first(a):
            return a.reg is None and a.off == 0

        def x1_bank(a, k):
            return (x_ps, pv_ps)[k][:] if is_first(a) else x_ps[:]

        def qk_bank(a, j):
            return (st_ps[:, 0], st_ps[:, 1], x_ps[:], pv_ps[:])[j] if is_first(a) else x_ps[:]

        def has_body(g):
            return ("Z1", 0) in [u[1:] for u in plan(g)]

        def has_end(g):
            return ("AT", 0) in [u[1:] for u in plan(g)]

        def s_fill(pe, u):
            wait(pe, y_taken[u % 2], u // 2)
            return y_ps[:, u % 2]

        def s_filled(eng, u):
            eng.wait_ge(y_full, u + 1)
            return y_ps[:, u % 2]

        def s_taken(eng, u):
            eng.wait_ge(y_taken[u % 2], u // 2 + 1)

        def in_chunk_order(ap):
            return ap.rearrange("p (mc d j) -> p mc j d", j=2, d=DH)

        def in_order(ap):
            return ap.rearrange("p (mc j d) -> p mc j d", j=2, d=DH)

        def head(c, r):
            return 8 * (r % 2) + 2 * c + r // 2

        def ln_bc(ap, n):
            return ap.unsqueeze(2).broadcast_to([P, ap.shape[1], n])

        block = ctx.enter_context(nc.Block())

        @block.sync
        def _(sp):
            def load_xa(a, row=None):
                wait_apart(sp, sp_passed, ln_out[0], a.times(4, 0))
                sp.dma_start(xa[:], x[(row or a).row()].rearrange("a (t p) d -> p (a t) d", p=P)).then_inc(xa_in, 16)

            def load_res(g):
                if g.reg is None and g.off == 0:
                    sp.wait_ge(y_full, SU_CTX + KT)
                else:
                    taken(sp, g + -1, "O", 2)
                    sp.sem_inc(sp_passed, 1)
                    taken(sp, g + -1, "O", 3)
                    sp.sem_inc(sp_passed, 1)
                sp.dma_start(res[:], x[g.row()].rearrange("a (t p) d -> p (a t) d", p=P)).then_inc(res_in, 16)

            def load_a(g, first=False):
                if first:
                    sp.wait_ge(as_out, 16 * 4 * PAIRS)
                else:
                    filled(sp, g + -1, "S", 7)
                    sp.sem_inc(sp_passed, 1)
                sp.dma_start(a_cat[:].bitcast(F32), a_scr[g.row()].rearrange("a p h k c -> (a p) h k c")).then_inc(a_in, 16)

            def load_b(g, first=False):
                if first:
                    sp.wait_ge(bs_out, 16 * PAIRS)
                else:
                    filled(sp, g + -1, "O", 3)
                    sp.sem_inc(sp_passed, 1)
                sp.dma_start(b_cat[:], b_scr[g.row()].rearrange("a p h c -> (a p) h c")).then_inc(b_in, 16)

            def fill_stack(a, c):
                wait_apart(sp, sp_passed, qk_taken, a.times(4, 4))
                wait(sp, st_full, (a + -1).times(TICKS, 16 * c + 16))
                for j, st, parts in ((0, q_st, (qk_hi, qk_hi, qk_lo)), (2, k_st, (qk_hi, qk_lo, qk_hi))):
                    for m in range(2):
                        for n, part in enumerate(parts):
                            p0 = 64 * m + DH * n
                            sp.dma_start(st[p0:p0 + DH, 2 * c:2 * c + 2, :].bitcast(F32),
                                         part[32 * c:32 * c + 32, j + m, :].bitcast(F32)).then_inc(refill[c], 16)

            def fill_maxrow(b, c):
                sp.wait_ge(sm_taken, b.times(CH * MAX_UNITS, MAX_UNITS * (c + 1)))
                for m in range(2):
                    for part in range(2):
                        p0 = 64 * m + S_MASK + part
                        sp.dma_start(q_st[p0:p0 + 1, 2 * c:2 * c + 2, :].bitcast(F32),
                                     nm[8 * m:8 * m + 8, c % 2, part, :].bitcast(F32)).then_inc(maxrow[c], 16)

            def load_pair(p):
                if p >= 2:
                    sp.wait_ge(y_full, SU_PAIR + PAIR_UNITS * (p - 1))
                else:
                    sp.wait_ge(y_full, SU_O1)
                cols = slice(P * p, P * p + P)
                t = w_st[:, p % 2]
                sp.dma_start(t[:, 0].rearrange("p (k c) -> p k c", k=KT),
                             xwq[:, cols].rearrange("(k p) c -> p k c", p=P)).then_inc(ws_in[p % 2], 16)
                sp.dma_start(t[:, 1].rearrange("p (k c) -> p k c", k=KT),
                             xwkv[:, cols].rearrange("(k p) c -> p k c", p=P)).then_inc(ws_in[p % 2], 16)
                sp.dma_start(t[:, 2].rearrange("p (k c) -> p k c", k=KT),
                             xwkv[:, INNER + P * p:INNER + P * p + P].rearrange("(k p) c -> p k c", p=P)
                             ).then_inc(ws_in[p % 2], 16)
                sp.dma_start(t[:, 3], xwo[cols, :]).then_inc(ws_in[p % 2], 16)

            def store_a(p, m):
                s_taken(sp, SU_PAIR + PAIR_UNITS * p + 3 + 2 * m)
                s_taken(sp, SU_PAIR + PAIR_UNITS * p + 4 + 2 * m)
                for part in range(2):
                    sp.dma_start(a_scr[:, :, part, m, P * p:P * p + P].rearrange("b p c -> p b c"),
                                 a_cat[:, part, m, :].bitcast(F32).rearrange("p (b c) -> p b c", b=B)
                                 ).then_inc(as_out, 16)

            def store_b(p):
                s_taken(sp, SU_PAIR + PAIR_UNITS * p + 9)
                s_taken(sp, SU_PAIR + PAIR_UNITS * p + 10)
                sp.dma_start(b_scr[:, :, p, :].rearrange("b p c -> p b c"), b_cat[:]).then_inc(bs_out, 16)

            for n, w in enumerate((wq, wk)):
                sp.dma_start(w_raw[:, n], w.rearrange("(f p) e -> p f e", p=P)).then_inc(qk_in, 16)
            load_xa(At(None, 0))
            sp.dma_start(brow[:, 0, :], bq.unsqueeze(0)).then_inc(qk_in, 16)
            sp.dma_start(brow[:, 1, :], bk.unsqueeze(0)).then_inc(qk_in, 16)
            sp.dma_start(bv_row[:], bv.unsqueeze(0)).then_inc(qk_in, 16)
            for n, w in ((2, wv), (3, wo)):
                sp.dma_start(w_raw[:, n], w.rearrange("(f p) e -> p f e", p=P)).then_inc(w_in, 16)
            sp.dma_start(wout1_raw, wout1.rearrange("(m p) r -> p m r", p=P)).then_inc(w_in, 16)
            sp.dma_start(wout2_raw, wout2.rearrange("(m p) r -> p m r", p=P)).then_inc(w_in, 16)
            sp.dma_start(bo_all[:], xbo.partition_broadcast(P)).then_inc(w_in, 16)
            sp.dma_start(gate_t[:, 0:1], gate.partition_broadcast(P)).then_inc(w_in, 16)
            sp.dma_start(ln_gb[:, 0, :], gamma.rearrange("(k p) -> p k", p=P), allow_slow_non_contiguous=True
                         ).then_inc(w_in, 16)
            sp.dma_start(ln_gb[:, 1, :], beta.rearrange("(k p) -> p k", p=P), allow_slow_non_contiguous=True
                         ).then_inc(w_in, 16)
            sp.dma_start(win1_f[:], win1[0:D, :].rearrange("(k p) r -> p k r", p=P)).then_inc(w_in, 16)
            sp.dma_start(zbias[:, 0:1], win1[D:D + 1, :].rearrange("a r -> r a")).then_inc(w_in, 16)
            sp.dma_start(proj_f[:], proj.rearrange("(k p) r -> p k r", p=P)).then_inc(w_in, 16)
            sp.dma_start(c12[:, 0, :], c1).then_inc(w_in, 16)
            sp.dma_start(c12[:, 1, :], c2).then_inc(w_in, 16)
            sp.dma_start(win2_f[:], win2[0:O, :].rearrange("(m p) r -> p m r", p=P)).then_inc(w_in, 16)
            sp.dma_start(zbias[:, 1:2], win2[O:O + 1, :].rearrange("a r -> r a")).then_inc(w_in, 16)
            sp.dma_start(ctx_raw[:], ctx_in.rearrange("(t a) s d -> (a s) t d", a=2)).then_inc(w_in, 16)
            sp.wait_ge(const_ready, CONSTS)
            for m in range(2):
                for st, row, kind in ((q_st, S_PROD, 0), (q_st, S_PROD + 1, 1), (k_st, S_PROD, 2),
                                      (k_st, S_PROD + 1, 3), (k_st, S_MASK, 4), (k_st, S_MASK + 1, 4)):
                    p0 = 64 * m + row
                    sp.dma_start(st[p0:p0 + 1, :, :].bitcast(F32),
                                 (ones_row.unsqueeze(1) if kind == 4 else mask_rows[:, kind:kind + 1, :])
                                 .broadcast_to([1, 2 * CH, N])).then_inc(rows_in, 16)
            load_pair(0)
            load_pair(1)
            load_xa(At(None, 1))
            for c in range(CH):
                fill_stack(At(None, 0), c)

            def swap_pair(p):
                store_a(p, 0)
                store_a(p, 1)
                store_b(p)
                if p + 2 < PAIRS:
                    load_pair(p + 2)

            for c in range(2):
                swap_pair(c)
                fill_maxrow(At(None, 0), c)

            def store(g):
                for n in range(2):
                    taken(sp, g + 1, "Y", n)
                    sp.sem_inc(sp_passed, 1)
                sp.dma_start(out[g.row()].rearrange("a (t p) d -> p (a t) d", p=P), res3[:]).then_inc(out_done, 16)

            def iteration(b, setup=False, store_=True, project=True, row=None):
                if project:
                    load_xa(b + 2, row)
                if store_:
                    store(b + -2)
                for c in range(CH):
                    if setup:
                        for p in ((2, 3), (4,), (5,), (6,))[c]:
                            swap_pair(p)
                    elif c == 3:
                        load_a(b)
                        load_b(b)
                        load_res(b)
                    if project:
                        fill_stack(b + 1, c)
                    if c < 2:
                        fill_maxrow(b, c + 2)
                    elif project:
                        fill_maxrow(b + 1, c - 2)
                if setup:
                    load_res(b)
                    swap_pair(PAIRS - 1)
                    load_a(b, first=True)
                    load_b(b, first=True)

            iteration(At(None, 0), setup=True, store_=False)
            iteration(At(None, 1), store_=False)
            with sp.Fori(2, B - 2) as it:
                iteration(At(it, 0))
            iteration(At(None, B - 2), row=At(None, B - 1))
            iteration(At(None, B - 1), project=False)
            store(At(None, B - 2))
            store(At(None, B - 1))
            sp.wait_ge(out_done, 16 * B)

        @block.tensor
        def _(pe):
            def mm(dst, lhs, rhs, start, stop, **kw):
                return nc.tensor.matmul(dst, lhs, rhs, start=start, stop=stop, **kw)

            def mm3(dst, pairs):
                last = None
                for n, (lh, ll, rh, rl) in enumerate(pairs):
                    end = n == len(pairs) - 1
                    mm(dst, lh, rh, n == 0, False)
                    mm(dst, lh, rl, False, False)
                    last = mm(dst, ll, rh, False, end)
                return last

            def scores(b, c, i, r):
                e = 16 * c + 4 * i + r
                if i == 0 and r == 0:
                    pe.wait_ge(maxrow[c], b.times(64, 64))
                wait(pe, exp_done, b.times(TICKS, e - 1))
                m, h = r % 2, 2 * c + r // 2
                rows_ = slice(64 * m, 64 * m + S_ALL)
                mm(st_ps[:, e % 2], k_st[rows_, h, P * i:P * i + P], q_st[rows_, h, :], True, True).then_inc(st_full, 1)

            def values(b, c, i):
                s = 4 * c + i
                pe.wait_ge(exp_done, b.times(TICKS, 4 * s + 4))
                if i == 0:
                    wait(pe, ot_done, b.times(CH, c))
                    if c == 0 and b.reg is None and b.off == 0:
                        s_taken(pe, SU_V)
                        s_taken(pe, SU_V + 1)
                    elif c == 0:
                        taken(pe, b + -1, "V", 0)
                        taken(pe, b + -1, "V", 1)
                for r in range(HC):
                    last = mm(pv_ps[VW * r:VW * r + VW, :], v_all[:, i, head(c, r), :], probs[:, s % 2, r, :],
                              i == 0, i == TT - 1, tile_position=(0, VW * r))
                last.then_inc(pv_done, 1)

            def for_max(b, c, i, r):
                u = MAX_UNITS * c + 4 * i + r
                if i == 0 and r == 0:
                    pe.wait_ge(refill[c], b.times(192, 192))
                wait(pe, sm_taken, b.times(CH * MAX_UNITS, u - 1))
                m, h = r % 2, 2 * c + r // 2
                rows_ = slice(64 * m, 64 * m + S_MASK)
                mm(sm_ps[:, u % 2], q_st[rows_, h, P * i:P * i + P], k_st[rows_, h, :], True, True).then_inc(sm_full, 1)

            def turn_max(b, c):
                u = MAX_UNITS * c + 16
                pe.wait_ge(sm_taken, b.times(CH * MAX_UNITS, u))
                mm(sm_ps[0:16, u % 2, 0:P], mx[:, c % 2, :], ident[:], True, True).then_inc(sm_full, 1)

            def turn_x1(a, k):
                pe.wait_ge(ln_out[0], a.times(4, 4))
                if a.reg is not None or a.off > 2:
                    wait(pe, pj_taken, a.times(1, -2))
                if not is_first(a):
                    wait(pe, t1_taken, a.times(2, k))
                for t in range(TT):
                    last = nc.tensor.transpose(x1_bank(a, k)[:, P * t:P * t + P], xn1[:, t, P * k:P * k + P], ident[:])
                last.then_inc(t1_full, 1)

            def qk(a, j):
                if j == 0:
                    wait(pe, t1_taken, a.times(2, 2))
                if not is_first(a):
                    wait(pe, qk_taken, a.times(4, j))
                cols = slice(P * (j % 2), P * (j % 2) + P)
                mm3(qk_bank(a, j), [(w_hi[:, j // 2, k, cols], w_lo[:, j // 2, k, cols], x1t_hi[:, k, :], x1t_lo[:, k, :])
                              for k in range(KT)]).then_inc(qk_full, 1)

            def v_tiles(y, n):
                for t in (2 * n, 2 * n + 1):
                    tok = slice(P * t, P * t + P)
                    last = mm3(y[:, D * (t % 2):D * (t % 2) + D],
                               [(x1t_hi[:, k, tok], x1t_lo[:, k, tok], w_hi[:, 2, k, :], w_lo[:, 2, k, :])
                                for k in range(KT)])
                last.then_inc(y_full, 1)

            def turn_o(g, t):
                pe.wait_ge(ot_done, g.times(4, 4))
                y = fill(pe, g, "OT", t)
                for c in range(CH):
                    last = nc.tensor.transpose(y[:, P * c:P * c + P], o_t[:, c, P * t:P * t + P], ident[:])
                last.then_inc(y_full, 1)

            def turn_xn(y, k):
                for t in range(TT):
                    last = nc.tensor.transpose(y[:, P * t:P * t + P], xn[:, t, P * k:P * k + P], ident[:])
                last.then_inc(y_full, 1)

            def out_proj(g, n):
                y = fill(pe, g, "WO", n, after=[("ON", 0), ("ON", 1)] if n == 0 else ())
                for t in (2 * n, 2 * n + 1):
                    tok = slice(P * t, P * t + P)
                    last = mm3(y[:, D * (t % 2):D * (t % 2) + D],
                               [(xt_hi[:, k, tok], xt_lo[:, k, tok], w_hi[:, 3, k, :], w_lo[:, 3, k, :])
                                for k in range(KT)])
                last.then_inc(y_full, 1)

            def x_scores(g, q, n):
                if q == 0 and n == 0:
                    pe.wait_ge(x2_lo, g.times(2, 2))
                    pe.wait_ge(a_in, g.times(16, 16))
                y = fill(pe, g, "S", 2 * q + n)
                tok, cols = slice(P * q, P * q + P), slice(N * n, N * n + N)
                mm3(y, [(xt_hi[:, k, tok], xt_lo[:, k, tok], a_cat[:, 0, k, cols], a_cat[:, 1, k, cols])
                        for k in range(KT)]).then_inc(y_full, 1)

            def x_turn(g, q, n):
                pe.wait_ge(c_norm, g.times(8, 2 * q + n + 1))
                y = fill(pe, g, "T", 2 * q + n)
                for p in range(4):
                    h = 8 * n + 2 * p
                    last = nc.tensor.transpose(y[:, P * p:P * p + P], px[:, q % 2, h:h + 2, :].rearrange("p h s -> p (h s)"),
                                               ident[:])
                last.then_inc(y_full, 1)

            def x_out(g, q):
                if q == 0:
                    pe.wait_ge(b_in, g.times(16, 16))
                y = fill(pe, g, "O", q, after=[("T", 2 * q), ("T", 2 * q + 1)])
                for p in range(PAIRS):
                    last = mm(y[:, 0:D], pt[:, q % 2, p, :], b_cat[:, p, :], p == 0, p == PAIRS - 1)
                last.then_inc(y_full, 1)

            def router(g):
                for k in range(KT):
                    taken(pe, g, "X3", k)
                if g.reg is not None or g.off + 2 < B:
                    pe.wait_ge(qk_taken, (g + 2).times(4, 4))
                wait(pe, z2_taken, g.times(1, 0))
                for t in range(TT):
                    tok = slice(P * t, P * t + P)
                    last = mm3(x_ps[:, E * t:E * t + E],
                               [(xt_hi[:, k, tok], xt_lo[:, k, tok], proj_hi[:, k, :], proj_lo[:, k, :])
                                for k in range(KT)])
                last.then_inc(pj_full, 1)

            def z1(g):
                y = fill(pe, g, "Z1", 0)
                mm3(y, [(win1_hi[:, k, :], win1_lo[:, k, :], xt_hi[:, k, :], xt_lo[:, k, :])
                        for k in range(KT)]).then_inc(y_full, 1)

            def turn_a(g):
                pe.wait_ge(en_step, g.times(EN, 0))
                y = fill(pe, g, "AT", 0)
                for t in range(TT):
                    last = mm(y[0:E, P * t:P * t + P], a_sb[:, t, :], ident[:], True, True)
                last.then_inc(y_full, 1)

            def gate_of(g, n):
                y = fill(pe, g, "G", n, after=[("AT", 0)])
                mm(y, c12[:, n, :], a_t, True, True).then_inc(y_full, 1)

            def up(g, m):
                if m == 0:
                    pe.wait_ge(zl, g.times(1, 0))
                    pe.wait_ge(pj_taken, g.times(1, 0))
                    if g.reg is not None or g.off + 2 < B:
                        pe.wait_ge(qk_taken, (g + 2).times(4, 4))
                y = fill(pe, g, "H", m)
                cols = slice(P * m, P * m + P)
                mm3(y, [(wout1_hi[:, cols], wout1_lo[:, cols], z_hi[:], z_lo[:])]).then_inc(y_full, 1)
                for k in ([m - 1] if m > 0 else []) + ([m] if m == O // P - 1 else []):
                    taken(pe, g, "H", k)
                    mm(x_ps[:], win2_f[:, k, :], h_t[:, k % 2, :], k == 0, k == O // P - 1).then_inc(z2_full, 1)

            def result(g, n):
                pe.wait_ge(z2_taken, g.times(1, 0))
                y = fill(pe, g, "Y", n)
                for t in (2 * n, 2 * n + 1):
                    last = mm(y[:, D * (t % 2):D * (t % 2) + D], z2g[:, P * t:P * t + P], wout2_t[:], True, True)
                last.then_inc(y_full, 1)

            def dense(g, t):
                for tick, kind, i in plan(g):
                    if tick != t:
                        continue
                    if kind == "V":
                        v_tiles(fill(pe, g, "V", i), i)
                    if kind == "OT":
                        turn_o(g, i)
                    if kind == "ON":
                        turn_xn(fill(pe, g, "ON", i, after=[("OT", 2), ("OT", 3)] if i == 0 else ()), i)
                    if kind == "WO":
                        out_proj(g, i)
                    if kind == "X2":
                        pe.wait_ge(ln_out[1], g.times(4, 4))
                        turn_xn(fill(pe, g, "X2", i), i)
                    if kind == "S":
                        x_scores(g, i // 2, i % 2)
                    if kind == "T":
                        x_turn(g, i // 2, i % 2)
                    if kind == "O":
                        x_out(g, i)
                    if kind == "X3":
                        pe.wait_ge(ln_out[2], g.times(4, 4))
                        turn_xn(fill(pe, g, "X3", i), i)
                    if kind == "Z1":
                        router(g)
                        z1(g)
                    if kind == "AT":
                        turn_a(g)
                    if kind == "G":
                        gate_of(g, i)
                    if kind == "H":
                        up(g, i)
                    if kind == "Y":
                        result(g, i)

            def projections(b, t):
                if t in X1_TICK:
                    turn_x1(b + 1, X1_TICK.index(t))
                if t in QK_TICK:
                    qk(b + 1, QK_TICK.index(t))

            def turn_pair(y, blocks):
                for f, block_ in enumerate(blocks):
                    last = nc.tensor.transpose(y[:, P * f:P * f + P], block_, ident[:])
                return last

            def setup_w(n):
                w, k = n // 2, n % 2
                y = s_fill(pe, SU_W[n])
                turn_pair(y, [w_raw[:, w, f, P * k:P * k + P] for f in range(2)]).then_inc(y_full, 1)

            def setup_bias():
                pe.wait_ge(small, 2)
                y = s_fill(pe, SU_BIAS)
                for j in range(4):
                    mm(y[:, j:j + 1], brow_c[:, j // 2, P * (j % 2):P * (j % 2) + P], ones_row[:, 0:1], True, True)
                for k in range(KT):
                    last = mm(y[:, 4 + k:5 + k], bv_row[:, P * k:P * k + P], ones_row[:, 0:1], True, True)
                last.then_inc(y_full, 1)

            def setup_wout():
                for n in range(2):
                    y = s_fill(pe, SU_O1 + n)
                    for m in range(4):
                        last = nc.tensor.transpose(y[:, P * m:P * m + P], wout1_raw[:, 4 * n + m, :], ident[:])
                    last.then_inc(y_full, 1)
                y = s_fill(pe, SU_O2)
                for m in range(2):
                    last = nc.tensor.transpose(y[:, P * m:P * m + P], wout2_raw[:, m, :], ident[:])
                last.then_inc(y_full, 1)

            def setup_ctx(k):
                y = s_fill(pe, SU_CTX + k)
                for t in range(TT):
                    last = nc.tensor.transpose(y[:, P * t:P * t + P], ctx_raw[:, t, P * k:P * k + P], ident[:])
                last.then_inc(y_full, 1)

            def setup_unit(p, n):
                u0 = SU_PAIR + PAIR_UNITS * p
                t = w_st[:, p % 2]
                y = s_fill(pe, u0 + n)
                if n == 0:
                    pe.wait_ge(ws_in[p % 2], 64 * (p // 2 + 1))
                    turn_pair(y, [t[:, 0, P * f:P * f + P] for f in range(2)]).then_inc(y_full, 1)
                if n in (1, 2):
                    for k in range(KT):
                        last = mm(y, t[:, n, P * k:P * k + P], ctx_t[:, k, :], k == 0, k == KT - 1)
                    last.then_inc(y_full, 1)
                if 3 <= n < 7:
                    m, j = (n - 3) // 2, (n - 3) % 2
                    hd = slice(XD * j, XD * j + XD)
                    mm(y, xwq_t[hd, p % 2, P * m:P * m + P], kv_t[hd, p % 2, 0, :], True, True).then_inc(y_full, 1)
                if n >= 7:
                    for b2 in range(2):
                        bb = 2 * (n - 7) + b2
                        for j in range(2):
                            hd = slice(XD * j, XD * j + XD)
                            last = mm(y[hd, D * b2:D * b2 + D], kv_t[hd, p % 2, 1, SK * bb:SK * bb + SK], t[hd, 3, :],
                                      True, True, tile_position=(XD * j, XD * j))
                    last.then_inc(y_full, 1)

            def setup(t):
                if t == 0:
                    setup_ctx(0)
                    setup_ctx(1)
                for n in range(PAIR_UNITS):
                    if t % 12 == PAIR_TICKS[n]:
                        setup_unit(t // 12, n)

            def iteration(b, project=True, has_setup=False):
                for c in range(CH):
                    for i in range(TT):
                        for r in range(HC):
                            t = 16 * c + 4 * i + r
                            scores(b, c, i, r)
                            if r == 1 and t > 4:
                                values(b, (t - 4) // 16, (t - 4) // 4 % 4)
                            if c < 2:
                                for_max(b, c + 2, i, r)
                            elif project:
                                for_max(b + 1, c - 2, i, r)
                            if project:
                                projections(b, t)
                            if has_setup:
                                setup(SETUP_TICKS + t)
                            else:
                                dense(b + -1, t)
                    if c < 2:
                        turn_max(b, c + 2)
                    elif project:
                        turn_max(b + 1, c - 2)
                values(b, CH - 1, TT - 1)

            first = At(None, 0)
            pe.wait_ge(const_ready, CONSTS)
            pe.wait_ge(qk_in, 16 * 5)
            for n in range(4):
                setup_w(n)
            setup_bias()
            for k in range(KT):
                turn_x1(first, k)
            pe.wait_ge(w_in, 16 * 16)
            setup_w(4)
            setup_w(5)
            for j in range(4):
                qk(first, j)
            setup_w(6)
            setup_w(7)
            setup_wout()
            pe.wait_ge(small, 6)
            for n in range(2):
                v_tiles(s_fill(pe, SU_V + n), n)
            pe.wait_ge(rows_in, 16 * 12)
            for c in range(2):
                for i in range(TT):
                    for r in range(HC):
                        for_max(first, c, i, r)
                        setup(16 * c + 4 * i + r)
                turn_max(first, c)
            iteration(first, has_setup=True)
            iteration(At(None, 1))
            with pe.Fori(2, B - 1) as it:
                iteration(At(it, 0))
            iteration(At(None, B - 1), project=False)
            for g in (B - 1, B):
                for t in range(TICKS):
                    dense(At(None, g), t)

        @block.scalar
        def _(act):
            def run(dst, src, f=ACT.Copy, **kw):
                return nc.scalar.activation(dst, src, f, **kw)

            def softmax_exp(b, t):
                act.wait_ge(st_full, b.times(TICKS, t + 1))
                if t % HC == 0:
                    wait(act, pv_done, b.times(16, t // HC - 1))
                run(probs[:, t // HC % 2, t % HC, :], st_ps[:, t % 2], ACT.Exp, scale=DH ** -0.5).then_inc(exp_done, 1)

            def save_chunk(b, c):
                act.wait_ge(pv_done, b.times(16, 4 * c + 4))
                if c == 0 and (b.reg is not None or b.off > 0):
                    filled(act, b + -1, "OT", TT - 1)
                run(o_t[:, c, :], pv_ps[:]).then_inc(ot_done, 1)

            def save_v(y, read, b, n):
                if n == 0:
                    wait(act, pv_done, b.times(16, 0))
                run(v_all[:, 2 * n:2 * n + 2, :, 0:DH], y.rearrange("p (t h d) -> p t h d", t=2, d=DH)
                    ).then_inc(read, 1)

            def x1_hi(a, k):
                if k == 0 and not is_first(a):
                    if a.reg is None and a.off == 1:
                        s_filled(act, SU_V + 1)
                    else:
                        filled(act, a + -2, "V", 1)
                act.wait_ge(t1_full, a.times(2, k + 1))
                run(x1t_hi[:, k, :], x1_bank(a, k)).then_inc(t1_hi, 1)

            def qk_hi_part(a, j):
                act.wait_ge(qk_full, a.times(4, j + 1))
                if j == 0:
                    for c in range(CH):
                        wait(act, refill[c], a.times(192, 0))
                run(qk_hi[:, j, :], qk_bank(a, j), ACT.Identity, bias=bqkv[:, j:j + 1]).then_inc(qk_hi_done, 1)

            def projections(b, t):
                if t in X1_TICK:
                    x1_hi(b + 1, X1_TICK.index(t))
                if t in QK_TICK:
                    qk_hi_part(b + 1, QK_TICK.index(t))

            def dense(g, t):
                for tick, kind, i in plan(g):
                    if tick != t or kind in ("OT", "WO", "S", "O", "Y"):
                        continue
                    if kind == "G" and i == 0:
                        continue
                    if kind == "H" and (i == 0 or FFN_TICK[i - 1] != tick):
                        run(table_pad[:, 1:2], table_pad[:, 0:1], ACT.Gelu)
                    y, read = filled(act, g, kind, i), done(g, kind, i)
                    if kind == "V":
                        save_v(y, read, g + 1, i)
                    if kind == "ON":
                        run(xt_hi[:, i, :], y, ACT.Identity, bias=bqkv[:, 4 + i:5 + i]).then_inc(on_hi, 1)
                    if kind == "X2":
                        gb = dict(scale=ln_gb[:, 0, i:i + 1], bias=ln_gb[:, 1, i:i + 1])
                        run(xt_hi[:, i, :], y, ACT.Identity, **gb)
                        run(xt_f[:, i, :], y, ACT.Identity, **gb).then_inc(read, 1)
                    if kind == "T":
                        q, n = i // 2, i % 2
                        run(pt[:, q % 2, 4 * n:4 * n + 4, :], y.rearrange("p (a b) -> p a b", b=P)).then_inc(read, 1)
                    if kind == "X3":
                        run(xt_hi[:, i, :], y).then_inc(x3_hi, 1)
                    if kind == "Z1":
                        run(z1s, y, ACT.Identity, bias=zbias[:, 0:1]).then_inc(read, 1)
                    if kind == "AT":
                        run(a_t, y[0:E, :]).then_inc(read, 1)
                    if kind == "G":
                        run(g2s, y).then_inc(read, 1)
                    if kind == "H":
                        if i >= 2:
                            act.wait_ge(z2_full, (g + -1).times(O // P, i - 1))
                        run(h_t[:, i % 2, :], y, ACT.Gelu).then_inc(read, 1)
                for q in range(TT):
                    for n in range(2):
                        if t == S_TICK[q][n] + 2 and ("S", 2 * q + n) in [u[1:] for u in plan(g)]:
                            taken(act, g, "S", 2 * q + n)
                            half_px = px[:, q % 2, 8 * n:8 * n + 8, :]
                            run(half_px, half_px, ACT.Exp, scale=XD ** -0.5).then_inc(c_exp, 1)
                if t == ZH_TICK and has_end(g):
                    taken(act, g, "G", 0)
                    run(z_hi[:], z1g).then_inc(zh, 1)

            def setup_unit(p, n):
                u = SU_PAIR + PAIR_UNITS * p + n
                y = s_filled(act, u)
                done = y_taken[u % 2]
                if n == 0:
                    run(xwq_t[:, p % 2, 0:D], y[:, 0:D]).then_inc(done, 1)
                if n in (1, 2):
                    run(kv_t[:, p % 2, n - 1, :], y).then_inc(done, 1)
                if 3 <= n < 7:
                    m, j = (n - 3) // 2, (n - 3) % 2
                    if n == 3:
                        wait(act, as_out, 64 * p)
                    run(a_cat[:, 0, m, :].rearrange("p (b j s) -> p b j s", b=B, j=2)[:, :, j, :],
                        y.rearrange("p (b s) -> p b s", b=B)).then_inc(w_hi_done, 1)
                if n >= 7:
                    if n == 7:
                        wait(act, bs_out, 16 * p)
                    run(b_cat[:, 2 * (n - 7):2 * (n - 7) + 2, :], y.rearrange("p (b f) -> p b f", b=2), ACT.Identity,
                        scale=gate_t[:, 1:2]).then_inc(done, 1)

            def setup(t):
                if t == 0:
                    for k in range(KT):
                        run(ctx_t[:, k, :], s_filled(act, SU_CTX + k)).then_inc(y_taken[k % 2], 1)
                for n in range(PAIR_UNITS):
                    if t % 12 == PAIR_TICKS[n]:
                        setup_unit(t // 12, n)

            def iteration(b, project=True, has_setup=False):
                for t in range(TICKS):
                    softmax_exp(b, t)
                    if t in (18, 34, 50):
                        save_chunk(b, t // 16 - 1)
                    if project:
                        projections(b, t)
                    if has_setup:
                        setup(SETUP_TICKS + t)
                    else:
                        dense(b + -1, t)
                save_chunk(b, CH - 1)

            def w_hi_part(n):
                y = s_filled(act, SU_W[n])[:, 0:D]
                dst = w_hi[:, n // 2, n % 2, :]
                if n < 4:
                    y, dst = in_order(y), in_chunk_order(dst)
                run(dst, y).then_inc(w_hi_done, 1)

            first = At(None, 0)
            for n in range(4):
                w_hi_part(n)
            run(bqkv[:], s_filled(act, SU_BIAS)[:, 0:6]).then_inc(y_taken[SU_BIAS % 2], 1)
            for k in range(KT):
                x1_hi(first, k)
            for n in (4, 5):
                w_hi_part(n)
            s_taken(act, SU_BIAS)
            for j in range(4):
                qk_hi_part(first, j)
            for n in (6, 7):
                w_hi_part(n)
            for n in range(2):
                run(wout1_hi[:, N * n:N * n + N], s_filled(act, SU_O1 + n)).then_inc(w_hi_done, 1)
            run(wout2_t[:], s_filled(act, SU_O2)[:, 0:D]).then_inc(y_taken[SU_O2 % 2], 1)
            for n in range(2):
                save_v(s_filled(act, SU_V + n), y_taken[n], first, n)
            act.wait_ge(w_in, 16 * 16)
            run(gate_t[:, 1:2], gate_t[:, 0:1], ACT.Tanh).then_inc(tanh_done, 1)
            act.wait_ge(tanh_done, 1)
            for t in range(SETUP_TICKS):
                setup(t)
            iteration(At(None, 0), has_setup=True)
            iteration(At(None, 1))
            with act.Fori(2, B - 1) as it:
                iteration(At(it, 0))
            iteration(At(None, B - 1), project=False)
            for g in (B - 1, B):
                for t in range(TICKS):
                    dense(At(None, g), t)

        @block.vector
        def _(dve):
            def minus(dst, a, b):
                return nc.vector.tensor_tensor(dst, a, b, ALU.subtract)

            def lo_part(dst, full, hi):
                return minus(dst, full, hi.bitcast(F32))

            def reduce_max(b, c, i, r):
                u = MAX_UNITS * c + 4 * i + r
                dve.wait_ge(sm_full, b.times(CH * MAX_UNITS, u + 1))
                col = 8 * (r % 2) + 4 * (r // 2) + i
                nc.vector.tensor_reduce(mx[:, c % 2, col:col + 1], sm_ps[:, u % 2], axis=AX, op=ALU.max
                                        ).then_inc(sm_taken, 1)

            def negate_max(b, c):
                u = MAX_UNITS * c + 16
                dve.wait_ge(sm_full, b.times(CH * MAX_UNITS, u + 1))
                if c >= 2:
                    dve.wait_ge(maxrow[c - 2], b.times(64, 64))
                else:
                    wait(dve, maxrow[c + 2], b.times(64, 0))
                src = sm_ps[0:16, u % 2, 0:P]
                nc.vector.tensor_scalar(nm[:, c % 2, 0, :], src, -1.0, None, ALU.mult).then_inc(nm_hi, 1)
                dve.wait_ge(nm_hi, b.times(CH, c + 1))
                nc.vector.scalar_tensor_tensor(out=nm[:, c % 2, 1, :], in0=src, scalar=-1.0,
                                               in1=nm[:, c % 2, 0, :].bitcast(F32), op0=ALU.mult, op1=ALU.subtract
                                               ).then_inc(sm_taken, 1)

            def ln_stats(n, src, b, tiles):
                for t in tiles:
                    nc.vector.bn_stats(stat[:, n, t, :], src[:, t, :]).then_inc(ln_stat[n], 1)

            def ln_moments(n, b):
                wait_apart(dve, dve_passed, ln_stat[n], b.times(8, 4))
                for t in range(TT):
                    nc.vector.bn_aggr(mv[:, n, t, :], stat[:, n, t, :]).then_inc(ln_stat[n], 1)
                dve.wait_ge(ln_stat[n], b.times(8, 8))
                mul, add = (1.0 + EPS, EPS * EPS) if n == 1 else (1.0, EPS)
                nc.vector.tensor_scalar(var[:, n, :], mv[:, n, :, 1], mul, add, ALU.mult, ALU.add).then_inc(ln_var[n], 1)

            def ln_apply(n, dst, src, b, tiles):
                if 0 in tiles:
                    dve.wait_ge(ln_rstd[n], b.times(1, 1))
                for t in tiles:
                    nc.vector.tensor_scalar(dst[:, t, :], src[:, t, :], mv[:, n, t, 0:1], rstd[:, n, t:t + 1],
                                            ALU.subtract, ALU.mult).then_inc(ln_out[n], 1)

            def ln1_a(a):
                dve.wait_ge(xa_in, a.times(16, 16))
                ln_stats(0, xa, a, range(TT))

            def ln1_b(a):
                wait(dve, t1_full, a.times(2, 0))
                ln_apply(0, xn1, xa, a, range(TT))

            def x1_lo(a, k):
                dve.wait_ge(t1_hi, a.times(2, k + 1))
                lo_part(x1t_lo[:, k, :], x1_bank(a, k), x1t_hi[:, k, :]).then_inc(t1_taken, 1)

            def qk_lo_part(a, j):
                dve.wait_ge(qk_hi_done, a.times(4, j + 1))
                nc.vector.scalar_tensor_tensor(out=qk_lo[:, j, :], in0=qk_bank(a, j), scalar=bqkv[:, j:j + 1],
                                               in1=qk_hi[:, j, :].bitcast(F32), op0=ALU.add, op1=ALU.subtract
                                               ).then_inc(qk_taken, 1)

            def projections(b, t):
                if t == LN1_TICK[0]:
                    ln1_a(b + 2)
                if t == LN1_TICK[1]:
                    ln_moments(0, b + 2)
                if t == LN1_TICK[2]:
                    ln1_b(b + 2)
                if t - 1 in X1_TICK:
                    x1_lo(b + 1, X1_TICK.index(t - 1))
                if t - 1 in QK_TICK:
                    qk_lo_part(b + 1, QK_TICK.index(t - 1))

            def heads_out(g, q):
                y = filled(dve, g, "OT", q).rearrange("p (h w) -> p h w", w=VW)
                nc.vector.reciprocal(rc[:, q, :], y[:, :, DH]).then_inc(rcp, 1)
                dve.wait_ge(rcp, g.times(4, q + 1))
                nc.vector.tensor_tensor(xn[:, q, :].rearrange("p (m cj d) -> p cj m d", m=2, d=DH),
                                        y[:, :, 0:DH].rearrange("p (cj m) d -> p cj m d", m=2),
                                        rc[:, q, :].rearrange("p (cj m) -> p cj m", m=2).unsqueeze(3)
                                        .broadcast_to([P, 2 * CH, 2, DH]), ALU.mult
                                        ).then_inc(done(g, "OT", q), 1)

            def add(dst, src, y, t0, n, read):
                nc.vector.tensor_tensor(dst[:, t0:t0 + n, :], y[:, 0:n * D].rearrange("p (t f) -> p t f", f=D),
                                        src[:, t0:t0 + n, :], ALU.add).then_inc(read, 1)

            def x_center(g, q, n):
                u = ("S", 2 * q + n)
                y = filled(dve, g, *u).rearrange("p (h s) -> p h s", s=SK)
                nc.vector.tensor_reduce(cst[:, n, 0, :], y, axis=AX, op=ALU.max).then_inc(c_max, 1)
                dve.wait_ge(c_max, g.times(8, 2 * q + n + 1))
                minus(px[:, q % 2, 8 * n:8 * n + 8, :], y, ln_bc(cst[:, n, 0, :], SK)).then_inc(done(g, *u), 1)

            def x_sums(g, q, n):
                k = 2 * q + n
                dve.wait_ge(c_exp, g.times(8, k + 1))
                nc.vector.tensor_reduce(cst[:, n, 1, :], px[:, q % 2, 8 * n:8 * n + 8, :], axis=AX, op=ALU.add
                                        ).then_inc(c_sum, 1)
                dve.wait_ge(c_sum, g.times(8, k + 1))
                wait(dve, c_norm, g.times(8, max(k - 1, 0)))
                nc.vector.reciprocal(cst[:, n, 2, :], cst[:, n, 1, :]).then_inc(c_rcp, 1)
                if is_last(g):
                    dve.wait_ge(c_rcp, g.times(8, k + 1))
                    x_divide(nc.vector, q, n).then_inc(c_norm, 1)

            en_n = [0]

            def step(ins):
                en_n[0] += 1
                ins.then_inc(en_step, 1)

            def entmax(g, part):
                V = nc.vector

                def after():
                    dve.wait_ge(en_step, g.times(EN, en_n[0]))

                def after_apart():
                    wait_apart(dve, dve_passed, en_step, g.times(EN, en_n[0]))

                def flat(ap):
                    return ap.rearrange("p a b -> p (a b)")

                if part == 0:
                    en_n[0] = 0
                    s = x_ps[:, 0:TT * E].rearrange("p (t e) -> p t e", e=E)
                    dve.wait_ge(pj_full, g.times(1, 1))
                    step(V.tensor_reduce(en_v[:, 0, :], s, axis=AX, op=ALU.add))
                    after()
                    V.scalar_tensor_tensor(out=en[:, 0], in0=ln_bc(en_v[:, 0, :], E), scalar=-1.0 / E, in1=s,
                                           op0=ALU.mult, op1=ALU.add).then_inc(pj_taken, 1)
                    dve.wait_ge(pj_taken, g.times(1, 1))
                    step(V.tensor_tensor(en[:, 1], en[:, 0], en[:, 0], ALU.mult))
                    step(V.tensor_reduce(en_v[:, 5, :], en[:, 0], axis=AX, op=ALU.max))
                    after()
                    step(V.tensor_reduce(en_v[:, 2, :], en[:, 1], axis=AX, op=ALU.add))
                    step(minus(en[:, 3], en[:, 0], ln_bc(en_v[:, 5, :], E)))
                    after()
                    step(V.tensor_scalar(en_v[:, 3, :], en_v[:, 2, :], 4.0 / E, 4.0 * EPS, ALU.mult, ALU.add))
                if part == 1:
                    after_apart()
                    for q in range(TT):
                        step(V.max(en_x[:, 0, q, 0:8], en[:, 3, q, :]))
                    after_apart()
                    for q in range(TT):
                        step(V.match_replace(en[:, 1, q, :], en_x[:, 0, q, 0:8], en[:, 3, q, :], -1e30))
                    after_apart()
                    for q in range(TT):
                        step(V.max(en_x[:, 0, q, 8:16], en[:, 1, q, :]))
                if part == 2:
                    dve.wait_ge(en_rstd, g.times(1, 1))
                    after()
                    step(V.tensor_tensor(en_s[:, 0], en_x[:, 0], ln_bc(en_v[:, 4, :], E), ALU.mult))
                    step(V.tensor_tensor(en[:, 0], en[:, 3], ln_bc(en_v[:, 4, :], E), ALU.mult))
                if part == 3:
                    after()
                    step(V.tensor_tensor(en_s[:, 1], en_s[:, 0], en_s[:, 0], ALU.mult))
                    after()
                    step(V.tensor_tensor_scan(en_c[:].rearrange("p a t e -> p (a t e)"),
                                              seg[:].rearrange("p a t e -> p (a t e)"),
                                              en_s[:].rearrange("p a t e -> p (a t e)"), 0.0, ALU.mult, ALU.add))
                    after()
                    step(V.tensor_tensor(en_m[:].rearrange("p a t e -> p a (t e)"),
                                         en_c[:].rearrange("p a t e -> p a (t e)"),
                                         flat(inv_ramp[:]).unsqueeze(1).broadcast_to([P, 2, TT * E]), ALU.mult))
                if part == 4:
                    after()
                    step(V.tensor_tensor(en[:, 1], en_m[:, 0], en_m[:, 0], ALU.mult))
                    step(minus(en[:, 3], en_m[:, 0], en_s[:, 0]))
                    after()
                    step(minus(en[:, 1], en[:, 1], en_m[:, 1]))
                    step(V.tensor_tensor(en[:, 3], en[:, 3], en[:, 3], ALU.mult))
                    after()
                    step(V.tensor_tensor(en[:, 1], en[:, 1], inv_ramp[:], ALU.add))
                    after()
                    step(V.tensor_scalar(en_m[:, 1], en[:, 1], 0.0, None, ALU.max))
                    after()
                    step(V.tensor_tensor(en[:, 3], en[:, 3], en_m[:, 1], ALU.is_le))
                    after()
                    step(V.tensor_reduce(en_v[:, 6, :], en[:, 3], axis=AX, op=ALU.add))
                if part == 5:
                    after()
                    step(V.tensor_tensor(en[:, 3], ramp[:], ln_bc(en_v[:, 6, :], E), ALU.is_equal))
                    after()
                    step(V.tensor_tensor(en_x[:].rearrange("p a t e -> p a (t e)"),
                                         en_m[:].rearrange("p a t e -> p a (t e)"),
                                         flat(en[:, 3]).unsqueeze(1).broadcast_to([P, 2, TT * E]), ALU.mult))
                    after()
                    step(V.tensor_reduce(en_v[:, 7:9, :], en_x[:], axis=AX, op=ALU.add))
                    after()
                    step(V.tensor_scalar(en_v[:, 3, :], en_v[:, 8, :], 1e-30, None, ALU.max))
                if part == 6:
                    dve.wait_ge(en_sqrt, g.times(1, 1))
                    step(minus(en_v[:, 5, :], en_v[:, 7, :], en_v[:, 9, :]))
                    after()
                    step(minus(en[:, 2], en[:, 0], ln_bc(en_v[:, 5, :], E)))
                    after()
                    step(V.scalar_tensor_tensor(out=a_sb[:], in0=en[:, 2], scalar=0.0, in1=en[:, 2],
                                                op0=ALU.max, op1=ALU.mult))
                    assert en_n[0] == EN, en_n[0]

            def dense(g, t):
                if has_end(g):
                    for n, tick in enumerate(EN_TICK):
                        if t == tick:
                            entmax(g + -1, 1 + n)
                    if t == G_TICK[0] + 1:
                        y = filled(dve, g, "G", 0)
                        taken(dve, g + -1, "Z1", 0)
                        nc.vector.tensor_tensor(z1g, y, z1s, ALU.mult).then_inc(done(g, "G", 0), 1)
                    if t == ZL_TICK:
                        dve.wait_ge(zh, g.times(1, 0))
                        lo_part(z_lo[:], z1g, z_hi[:]).then_inc(zl, 1)
                    if t == Z2_TICK:
                        dve.wait_ge(z2_full, g.times(O // P, 0))
                        taken(dve, g, "G", 1)
                        nc.vector.scalar_tensor_tensor(out=z2g, in0=x_ps[:], scalar=zbias[:, 1:2], in1=g2s,
                                                       op0=ALU.add, op1=ALU.mult).then_inc(z2_taken, 1)
                for tick, kind, i in plan(g):
                    if tick != t - 1:
                        continue
                    y, read = y_of(g, kind, i), done(g, kind, i)
                    if kind == "OT":
                        heads_out(g, i)
                    if kind == "ON":
                        dve.wait_ge(on_hi, g.times(2, i + 1))
                        nc.vector.scalar_tensor_tensor(out=xt_lo[:, i, :], in0=y, scalar=bqkv[:, 4 + i:5 + i],
                                                       in1=xt_hi[:, i, :].bitcast(F32), op0=ALU.add, op1=ALU.subtract
                                                       ).then_inc(read, 1)
                    if kind == "WO":
                        if i == 0:
                            dve.wait_ge(res_in, g.times(16, 16))
                        add(res, res, filled(dve, g, kind, i), 2 * i, 2, read)
                    if kind == "X2":
                        taken(dve, g, kind, i)
                        lo_part(xt_lo[:, i, :], xt_f[:, i, :], xt_hi[:, i, :]).then_inc(x2_lo, 1)
                    if kind == "S":
                        x_center(g, i // 2, i % 2)
                    if kind == "O":
                        if i == 0:
                            dve.wait_ge(bo_added, g.times(1, 1))
                            wait(dve, out_done, g.times(16, 0))
                        add(res3, res, filled(dve, g, kind, i), i, 1, read)
                    if kind == "X3":
                        dve.wait_ge(x3_hi, g.times(2, i + 1))
                        lo_part(xt_lo[:, i, :], y, xt_hi[:, i, :]).then_inc(read, 1)
                    if kind == "Y":
                        add(res3, res3, filled(dve, g, kind, i), 2 * i, 2, read)
                if has_body(g):
                    for n in range(2):
                        if t == WO_TICK[n] + 2:
                            taken(dve, g, "WO", n)
                            ln_stats(1, res, g, (2 * n, 2 * n + 1))
                    if t == LN2_TICK[0]:
                        ln_moments(1, g)
                    if t == LN2_TICK[1]:
                        ln_apply(1, xn, res, g, (0, 1))
                    if t == LN2_TICK[2]:
                        ln_apply(1, xn, res, g, (2, 3))
                    for q in range(TT):
                        for n in range(2):
                            if t == SUM_TICK[q][n]:
                                x_sums(g, q, n)
                        if t == O_TICK[q] + 2:
                            taken(dve, g, "O", q)
                            ln_stats(2, res3, g, (q,))
                    if t == LN3_TICK[0]:
                        ln_moments(2, g)
                    if t == LN3_TICK[1]:
                        ln_apply(2, xn, res3, g, range(TT))
                    if t == Z1_TICK + 1:
                        entmax(g, 0)

            def setup(t):
                p = t // 12
                for n in range(3, 7):
                    if t % 12 == PAIR_TICKS[n]:
                        m, j = (n - 3) // 2, (n - 3) % 2
                        u = SU_PAIR + PAIR_UNITS * p + n
                        dve.wait_ge(w_hi_done, 10 + 4 * p + n - 2)
                        if n == 3:
                            wait(dve, as_out, 64 * p)
                        dst, hi = (a_cat[:, part, m, :].rearrange("p (b j s) -> p b j s", b=B, j=2)[:, :, j, :]
                                   for part in (1, 0))
                        lo_part(dst, y_ps[:, u % 2].rearrange("p (b s) -> p b s", b=B), hi).then_inc(y_taken[u % 2], 1)

            def iteration(b, project=True, has_setup=False):
                for t in range(TICKS):
                    c, i, r = t // 16, t // 4 % 4, t % 4
                    if c < 2:
                        reduce_max(b, c + 2, i, r)
                    elif project:
                        reduce_max(b + 1, c - 2, i, r)
                    if project:
                        projections(b, t)
                    if has_setup:
                        setup(SETUP_TICKS + t)
                    else:
                        dense(b + -1, t)
                    if r == 3 and i == 3:
                        if c < 2:
                            negate_max(b, c + 2)
                        elif project:
                            negate_max(b + 1, c - 2)

            def w_lo_part(n):
                u = SU_W[n]
                dve.wait_ge(w_hi_done, n + 1)
                y, dst, hi = y_ps[:, u % 2, 0:D], w_lo[:, n // 2, n % 2, :], w_hi[:, n // 2, n % 2, :]
                if n < 4:
                    y, dst, hi = in_order(y), in_chunk_order(dst), in_chunk_order(hi)
                lo_part(dst, y, hi).then_inc(y_taken[u % 2], 1)

            first, second = At(None, 0), At(None, 1)
            dve.wait_ge(qk_in, 16 * 5)
            for n in range(2):
                nc.vector.tensor_copy(in_chunk_order(brow_c[:, n, :]), in_order(brow[:, n, :])).then_inc(small, 1)
            ln1_a(first)
            ln_moments(0, first)
            for n in range(4):
                w_lo_part(n)
            ln1_b(first)
            for k in range(KT):
                x1_lo(first, k)
            for n in (4, 5):
                w_lo_part(n)
            s_taken(dve, SU_BIAS)
            for j in range(4):
                qk_lo_part(first, j)
            for n in (6, 7):
                w_lo_part(n)
            for n in range(2):
                u = SU_O1 + n
                dve.wait_ge(w_hi_done, 9 + n)
                lo_part(wout1_lo[:, N * n:N * n + N], y_ps[:, u % 2], wout1_hi[:, N * n:N * n + N]
                        ).then_inc(y_taken[u % 2], 1)
            dve.wait_ge(w_in, 16 * 16)
            nc.vector.tensor_copy(win1_hi[:], win1_f[:]).then_inc(small, 1)
            nc.vector.tensor_copy(proj_hi[:], proj_f[:]).then_inc(small, 1)
            dve.wait_ge(small, 4)
            lo_part(win1_lo[:], win1_f[:], win1_hi[:]).then_inc(small, 1)
            lo_part(proj_lo[:], proj_f[:], proj_hi[:]).then_inc(small, 1)
            ln1_a(second)
            ln_moments(0, second)
            dve.wait_ge(const_ready, CONSTS)
            for c in range(2):
                for i in range(TT):
                    for r in range(HC):
                        reduce_max(first, c, i, r)
                        setup(16 * c + 4 * i + r)
                negate_max(first, c)
                if c == 0:
                    ln1_b(second)
            iteration(first, has_setup=True)
            iteration(At(None, 1))
            with dve.Fori(2, B - 1) as it:
                iteration(At(it, 0))
            iteration(At(None, B - 1), project=False)
            for g in (B - 1, B):
                for t in range(TICKS):
                    dense(At(None, g), t)

        @block.gpsimd
        def _(gp):
            G = nc.gpsimd

            def const(ins):
                ins.then_inc(const_ready, 1)

            def deviation(n, b):
                gp.wait_ge(ln_var[n], b.times(1, 1))
                G.tensor_tensor(rstd[:, n, :], var[:, n, :], half[:, 0, :], ALU.pow).then_inc(ln_rstd[n], 1)

            def entmax_powers(g):
                gp.wait_ge(en_step, g.times(EN, EN_VAR))
                G.tensor_tensor(en_v[:, 4, :], en_v[:, 3, :], half[:, 0, :], ALU.pow).then_inc(en_rstd, 1)
                gp.wait_ge(en_step, g.times(EN, EN_DELTA))
                G.tensor_tensor(en_v[:, 9, :], en_v[:, 3, :], half[:, 1, :], ALU.pow).then_inc(en_sqrt, 1)

            def dense(g, project=True):
                deviation(1, g)
                gp.wait_ge(ln_out[1], g.times(4, 4))
                G.tensor_tensor(res[:], res[:], bo_all[:].unsqueeze(1).broadcast_to([P, TT, D]), ALU.add
                                ).then_inc(bo_added, 1)
                for q in range(0 if is_last(g) else TT):
                    for n in range(2):
                        gp.wait_ge(c_rcp, g.times(8, 2 * q + n + 1))
                        x_divide(G, q, n).then_inc(c_norm, 1)
                if project:
                    deviation(0, g + 3)
                deviation(2, g)

            const(G.memset(ident[:], 0.0))
            const(G.memset(table_pad[:, 0:1], 0.0))
            const(G.memset(half[:, 0, :], -0.5))
            const(G.memset(half[:, 1, :], 0.5))
            const(G.memset(mask_rows, 0.0))
            const(G.memset(seg[:], 1.0))
            const(G.memset(v_all[:, :, :, DH:VW], 1.0))
            for k in range(E):
                const(G.memset(ramp[:, :, k:k + 1], float(k + 1)))
                const(G.memset(inv_ramp[:, :, k:k + 1], 1.0 / (k + 1)))
            gp.wait_ge(const_ready, 7 + 2 * E)
            const(G.affine_select(out=ident[:], in_=ident[:], compare_op=ALU.not_equal, fill=1.0, base=0,
                                  pattern=[[-1, P]], channel_multiplier=1))
            const(G.memset(mask_rows[:, 0, 0:1], 1.0))
            const(G.memset(mask_rows[:, 1, N - 1:N], 1.0))
            const(G.memset(mask_rows[:, 2, N - 1:N], NEG))
            const(G.memset(mask_rows[:, 3, 0:1], NEG))
            const(G.memset(ones_row, 1.0))
            const(G.memset(seg[:, :, :, 0:1], 0.0))
            deviation(0, At(None, 0))
            gp.wait_ge(tanh_done, 1)
            G.tensor_scalar(bo_all[:], bo_all[:], gate_t[:, 1:2], None, ALU.mult).then_inc(bo_done, 1)
            gp.wait_ge(bo_done, 1)
            deviation(0, At(None, 1))
            deviation(0, At(None, 2))
            dense(At(None, 0))
            with gp.Fori(2, B - 1) as it:
                entmax_powers(At(it, -2))
                dense(At(it, -1))
            for g in (B - 2, B - 1):
                entmax_powers(At(None, g - 1))
                dense(At(None, g), project=False)
            entmax_powers(At(None, B - 1))


_INS = ["x", "ctx_1024", "L0_attn_Wq", "L0_attn_bq", "L0_attn_Wk", "L0_attn_bk", "L0_attn_Wv", "L0_attn_bv",
        "L0_attn_Wo", "L0_xattn_ln_gamma", "L0_xattn_ln_beta", "L0_xattn_w_q", "L0_xattn_w_kv", "L0_xattn_w_out",
        "L0_xattn_b_out", "L0_xattn_gate", "L0_ffn_proj", "L0_ffn_C1", "L0_ffn_Win1", "L0_ffn_Wout1", "L0_ffn_C2",
        "L0_ffn_Win2", "L0_ffn_Wout2"]


def kernel(**inputs):
    import concourse.bacc as bacc
    from concourse.bass_utils import run_bass_kernel_spmd

    nc = bacc.Bacc("TRN2", target_bir_lowering=False, num_devices=1)
    arrays, args = {}, []
    for name in _INS:
        a = np.ascontiguousarray(inputs[name])
        arrays[f"in_{name}"] = a
        args.append(nc.dram_tensor(f"in_{name}", a.shape, F32, kind="ExternalInput").ap())
    out = nc.dram_tensor("out_x", (B, N, D), F32, kind="ExternalOutput").ap()
    a_scr = nc.dram_tensor("a_scr", (B, P, 2, KT, INNER), F32, kind="Internal").ap()
    b_scr = nc.dram_tensor("b_scr", (B, P, PAIRS, D), F32, kind="Internal").ap()
    build_kernel(nc, *args, out, a_scr, b_scr)
    r = run_bass_kernel_spmd(nc, [arrays], core_ids=[0])
    return r.results[0]["out_x"]
```
